# Optimizing a Trainium2 kernel written in Bass

```python
import numpy as np
import jax
import jax.numpy as jnp

def _softmax(x, axis=-1):
    return jax.nn.softmax(x, axis=axis)

def _gelu(x):
    return jax.nn.gelu(x, approximate=True)

def _silu(x):
    return jax.nn.silu(x)

def _sigmoid(x):
    return jax.nn.sigmoid(x)

def _layernorm(x, axis=-1, eps=1e-05):
    m = jnp.mean(x, axis=axis, keepdims=True)
    v = jnp.var(x, axis=axis, keepdims=True)
    return (x - m) / jnp.sqrt(v + eps)

def _scatter_add(tgt, idx, src, axis=0):
    return tgt.at[idx].add(src)

def _segment_sum(src, seg, n):
    return jax.ops.segment_sum(src, seg, n)
kernel_name = 'mk_recurrent_d1_jaxref_r8_1c3a9b'

def setup_inputs(seed: int=0):
    np.random.seed(seed)
    _w = jnp.asarray

    def _L0_attn_setup():
        import jax, jax.numpy as jnp
        import numpy as np
        B, S, EMB = (2, 256, 512)
        NHEADS, KVHEADS, HEAD_D = (32, 8, 128)
        SPLITS = (NHEADS * HEAD_D, KVHEADS * HEAD_D, KVHEADS * HEAD_D)
        key = jax.random.key(seed)
        k1, k2, k3 = jax.random.split(key, 3)
        q = jax.random.normal(k1, (B, S, EMB), dtype=jnp.float32)
        w_qkv = jax.random.normal(k2, (sum(SPLITS), EMB), dtype=jnp.float32) * 0.02
        w_dense = jax.random.normal(k3, (EMB, NHEADS * HEAD_D), dtype=jnp.float32) * 0.02
        return {'q': q, 'w_qkv': w_qkv, 'w_dense': w_dense}
    _L0_attn_in = _L0_attn_setup()

    def _L0_ffn_setup():
        import jax, jax.numpy as jnp
        import numpy as np
        import math
        D = 512
        TOKENS = (4, 256)
        P = 0.8

        def conn_dense(kernel, x):
            w = jnp.where(kernel, jnp.asarray(1.0, x.dtype), jnp.asarray(-1.0, x.dtype))
            return x @ w

        def ei_dense(x, kernel, scale, p):
            in_dim = x.shape[-1]
            ne = round(in_dim * p)
            x_exc = x[..., :ne]
            x_inh = x[..., ne:]
            xx = jnp.concatenate([x_exc, -p / (1.0 - p) * x_inh], axis=-1)
            return scale * conn_dense(kernel, xx)
        key = jax.random.key(seed)
        ks = jax.random.split(key, 4)
        x = jax.random.normal(ks[0], (*TOKENS, D), dtype=jnp.float32)
        k0 = jax.random.bernoulli(ks[1], 0.5, (D, D))
        k1 = jax.random.bernoulli(ks[2], 0.5, (D, D))
        k2 = jax.random.bernoulli(ks[3], 0.5, (D, D))
        s = jnp.asarray(1.0 / math.sqrt(D), dtype=jnp.float32)
        return {'x': x, 'k0': k0, 's0': s, 'k1': k1, 's1': s, 'k2': k2, 's2': s}
    _L0_ffn_in = _L0_ffn_setup()
    _d = {'L0_attn_q': _L0_attn_in['q'], 'L0_attn_w_qkv': _L0_attn_in['w_qkv'], 'L0_attn_w_dense': _L0_attn_in['w_dense'], 'L0_ffn_k0': _L0_ffn_in['k0'], 'L0_ffn_s0': _L0_ffn_in['s0'], 'L0_ffn_k1': _L0_ffn_in['k1'], 'L0_ffn_s1': _L0_ffn_in['s1'], 'L0_ffn_k2': _L0_ffn_in['k2'], 'L0_ffn_s2': _L0_ffn_in['s2']}
    _x0 = _d['L0_attn_q']
    _d['L0_attn_q'] = jax.random.normal(jax.random.fold_in(jax.random.key(seed), 1), (1, 1024, 512), dtype=_x0.dtype)
    del _x0
    return _d

def reference(L0_attn_q, L0_attn_w_qkv, L0_attn_w_dense, L0_ffn_k0, L0_ffn_s0, L0_ffn_k1, L0_ffn_s1, L0_ffn_k2, L0_ffn_s2):

    def _L0_attn_ref(q, w_qkv, w_dense):
        import jax, jax.numpy as jnp
        import numpy as np
        B, S, EMB = (2, 256, 512)
        NHEADS, KVHEADS, HEAD_D = (32, 8, 128)
        SPLITS = (NHEADS * HEAD_D, KVHEADS * HEAD_D, KVHEADS * HEAD_D)
        Bq, Sq, _ = q.shape
        qkv = q @ w_qkv.T
        qs, ks, vs = jnp.split(qkv, np.cumsum(SPLITS)[:-1], axis=-1)
        G = NHEADS // KVHEADS
        qh = qs.reshape(Bq, Sq, KVHEADS, G, HEAD_D)
        kh = ks.reshape(Bq, Sq, KVHEADS, HEAD_D)
        vh = vs.reshape(Bq, Sq, KVHEADS, HEAD_D)
        scale = 1.0 / jnp.sqrt(jnp.float32(HEAD_D))
        scores = jnp.einsum('bskgd,btkd->bkgst', qh, kh) * scale
        causal = jnp.tril(jnp.ones((Sq, Sq), dtype=bool))
        scores = jnp.where(causal, scores, jnp.finfo(scores.dtype).min)
        probs = jax.nn.softmax(scores, axis=-1)
        attn = jnp.einsum('bkgst,btkd->bskgd', probs, vh)
        attn = attn.reshape(Bq, Sq, NHEADS * HEAD_D)
        return attn @ w_dense.T

    def _L0_ffn_ref(x, k0, s0, k1, s1, k2, s2):
        import jax, jax.numpy as jnp
        import numpy as np
        import math
        D = 512
        TOKENS = (4, 256)
        P = 0.8

        def conn_dense(kernel, x):
            w = jnp.where(kernel, jnp.asarray(1.0, x.dtype), jnp.asarray(-1.0, x.dtype))
            return x @ w

        def ei_dense(x, kernel, scale, p):
            in_dim = x.shape[-1]
            ne = round(in_dim * p)
            x_exc = x[..., :ne]
            x_inh = x[..., ne:]
            xx = jnp.concatenate([x_exc, -p / (1.0 - p) * x_inh], axis=-1)
            return scale * conn_dense(kernel, xx)
        h = s0 * conn_dense(k0, x)
        h = jax.nn.relu(h) * 2.0
        h = ei_dense(h, k1, s1, P)
        h = jax.nn.relu(h) * 2.0
        return ei_dense(h, k2, s2, P)
    x = L0_attn_q
    xn = _layernorm(x, axis=-1)
    s = _L0_attn_ref(xn, L0_attn_w_qkv, L0_attn_w_dense)
    g = _silu(_L0_ffn_ref(xn, L0_ffn_k0, L0_ffn_s0, L0_ffn_k1, L0_ffn_s1, L0_ffn_k2, L0_ffn_s2))
    x = x + s * g
    return x

_drawn_inputs = setup_inputs


def setup_inputs(seed=0):
    import zlib

    import numpy as np

    out = dict(_drawn_inputs(seed))
    spreads = {}
    factors = {}
    for name, (base, spread) in spreads.items():
        noise = np.random.default_rng([zlib.crc32(name.encode()), seed]).standard_normal(out[name].shape)
        drawn = base * np.exp(spread * noise) if base else spread * noise
        out[name] = jnp.asarray(drawn.astype(out[name].dtype))
    for name, factor in factors.items():
        out[name] = (out[name] * factor).astype(out[name].dtype)
    return out
```

```python
from contextlib import ExitStack

import concourse.bass as bass
from concourse import mybir

F32 = mybir.dt.float32
F32R = mybir.dt.float32r
BF16 = mybir.dt.bfloat16
U8 = mybir.dt.uint8
ACT = mybir.ActivationFunctionType
ALU = mybir.AluOpType
AX_X = mybir.AxisListType.X

P = 128
S, E = 1024, 512
GROUPS, HEADS = 8, 4
BLOCKS = S // P
CHUNKS = E // P
HALF = S // 2
EPS = 1e-5
SCALE = float(P) ** -0.5
MASKED = -1e37
EXC = round(E * 0.8)
INH_FACTOR = -0.8 / (1.0 - 0.8)

RAW = 5
SCORE_RING = 2
TURN_RING = 2
PT_RING = 4
ATTN_RING = 2
STAT_RING = 8
LAG = 2

PIECES = ["q0", "q1", "q2", "q3", "v", "k"]
PRO_PIECES = len(PIECES)
BODY_PIECES = HEADS + PRO_PIECES


def tri(i):
    return i * (i + 1) // 2


TURNS = tri(BLOCKS)
SCORES = HEADS * BLOCKS


def merge(first, second):
    total = [max(1, sum(c for c, _ in part)) for part in (first, second)]
    done, at, out = [0.0, 0.0], [0, 0], []
    parts = (first, second)
    while at[0] < len(first) or at[1] < len(second):
        n = 0 if at[1] == len(second) or (at[0] < len(first) and done[0] <= done[1]) else 1
        cost, item = parts[n][at[n]]
        out.append(item)
        done[n] += cost / total[n]
        at[n] += 1
    return out


def step_items(s, last):
    scores = [(3 * max(s + 2, 2) / 4, ("scores", s + 1, h)) for h in range(HEADS)]
    dense = [(12, ("dense", s - 1))]
    unit = lambda piece, half: (12, ("unit", piece, half))
    split = lambda *pieces: [(0, ("split", p)) for p in pieces]
    nxt = not last
    rest = {
        0: scores + [unit("q0", 1), unit("q1", 1)] + split("wd0", "wd1", "wd2", "wd3"),
        1: scores + dense + [unit("k", 1), unit("q2", 1)] + (split("q0", "q1") if nxt else []),
        2: scores + dense + [unit("q3", 1), unit("v", 1)] + (split("q2") if nxt else []),
        3: scores + [(4, ("vblocks", 1))] + (split("q3", "v", "k") if nxt else []) + dense
        + ([unit("q0", 0)] if nxt else []),
        4: scores + dense + ([unit("q1", 0)] if nxt else []),
        5: scores + dense + ([unit("q2", 0)] if nxt else []),
        6: scores + dense + ([unit("q3", 0), unit("v", 0)] if nxt else []),
        7: ([unit("k", 0)] if nxt else []) + dense
        + ([(1.5, ("scores", 0, h)) for h in range(HEADS)] if nxt else []),
    }[s]
    walk = []
    for j in range(s + 1 + LAG):
        if j <= s:
            walk.append((4, ("turn", s, j)))
        if j >= LAG:
            walk.append((3, ("weigh", s, j - LAG)))
    items = merge(walk, rest)
    if s == BLOCKS - 1:
        items += ([("vblocks", 0)] if nxt else []) + [("dense", s)]
    return items


def with_inverses(items):
    out, due = [], []
    for n, item in enumerate(items):
        out.append(item)
        out += [("inverse", *s[1:]) for at, s in due if at == n]
        if item[0] == "scores":
            due.append((n + 2, item))
    return out + [("inverse", *s[1:]) for at, s in due if at >= len(items)]


PROLOGUE = ([("split", p) for p in PIECES] + [("unit", p, 0) for p in PIECES]
            + [("scores", 0, h) for h in range(HEADS)] + [("vblocks", 0)])
PROLOGUE = with_inverses(PROLOGUE)
BODY = with_inverses([item for s in range(BLOCKS) for item in step_items(s, False)])
LAST = with_inverses([item for s in range(BLOCKS) for item in step_items(s, True)])


def shared(items):
    return [i for i in items if i[0] in ("unit", "vblocks", "dense")]


def has_hi(item):
    return item[0] == "vblocks" or (item[0] == "unit" and item[1] != "v")


PRO_SHARED, BODY_SHARED = len(shared(PROLOGUE)), len(shared(BODY))
PRO_HI = sum(map(has_hi, shared(PROLOGUE)))
BODY_HI = sum(map(has_hi, shared(BODY)))


class Runs:

    def __init__(self, items, g):
        self.items, self.g = items, g
        pro = items is PROLOGUE
        self.shared0 = 0 if pro else PRO_SHARED + BODY_SHARED * g
        self.hi0 = 0 if pro else PRO_HI + BODY_HI * g
        self.piece0 = 0 if pro else PRO_PIECES + BODY_PIECES * g
        self.order = shared(items)
        self.his = [i for i in self.order if has_hi(i)]
        self.splits = [i[1] for i in items if i[0] == "split"]

    def shared_no(self, item):
        return self.shared0 + self.order.index(item) + 1

    def hi_no(self, item):
        return self.hi0 + self.his.index(item) + 1

    def piece_no(self, piece):
        return self.piece0 + self.splits.index(piece) + 1

    def group_of_scores(self, block):
        return self.g + 1 if block == 0 else self.g


def raw_slot(pro, n):
    return (n if pro else PRO_PIECES + n) % RAW


def raw_turn(pro, n, g):
    return n // RAW + 1 if pro else (PRO_PIECES + n) // RAW + 1 + BODY_PIECES // RAW * g


def build(nc, x_d, wqkv_d, wd_d, k_ds, s_ds, out_d):
    assert BODY_PIECES % RAW == 0 and SCORES % SCORE_RING == 0
    assert TURNS % TURN_RING == 0 and TURNS % PT_RING == 0
    ctx = ExitStack()
    with ctx:
        def sb(name, shape, dt=F32):
            return ctx.enter_context(nc.sbuf_tensor(name, shape, dt))

        def ps(name, shape):
            return ctx.enter_context(nc.psum_tensor(name, shape, F32))

        def sem(name):
            return ctx.enter_context(nc.semaphore(name))

        xn_hi = sb("xn_hi", [P, CHUNKS, S], F32R)
        xn_lo = sb("xn_lo", [P, CHUNKS, S], F32R)
        y = sb("y", [P, BLOCKS, E])
        raw = sb("raw", [P, RAW, E])
        w_hi = sb("w_hi", [P, PRO_PIECES, CHUNKS, P], F32R)
        w_lo = sb("w_lo", [P, PRO_PIECES, CHUNKS, P], F32R)
        wd_hi = sb("wd_hi", [P, HEADS, E], F32R)
        wd_lo = sb("wd_lo", [P, HEADS, E], F32R)
        q_hi = sb("q_hi", [P, HEADS, S], F32R)
        q_lo = sb("q_lo", [P, HEADS, S], F32R)
        k_hi = sb("k_hi", [P, S], F32R)
        k_lo = sb("k_lo", [P, S], F32R)
        vt = sb("vt", [P, S])
        v_hi = sb("v_hi", [P, BLOCKS, P], F32R)
        v_lo = sb("v_lo", [P, BLOCKS, P], F32R)
        prob_even = sb("prob_even", [P, HEADS, S - P])
        prob_odd = sb("prob_odd", [P, HEADS, S])
        pt_hi = sb("pt_hi", [P, PT_RING, HEADS, P], F32R)
        pt_lo = sb("pt_lo", [P, PT_RING, HEADS, P], F32R)
        at_hi = sb("at_hi", [P, ATTN_RING, HEADS, P], F32R)
        at_lo = sb("at_lo", [P, ATTN_RING, HEADS, P], F32R)
        ident = sb("ident", [P, P])
        ident_b = sb("ident_b", [P, P], BF16)
        mask_b = sb("mask_b", [P, P], BF16)
        neg_max = sb("neg_max", [P, STAT_RING])
        row_sum = sb("row_sum", [P, STAT_RING])
        row_inv = sb("row_inv", [P, STAT_RING])
        bn = sb("bn", [P, BLOCKS, 6])
        mv = sb("mv", [P, BLOCKS, 2])
        var_eps = sb("var_eps", [P, BLOCKS])
        std = sb("std", [P, BLOCKS])
        rstd = sb("rstd", [P, BLOCKS])
        newton = sb("newton", [P, BLOCKS])
        scales = sb("scales", [P, 3])
        scales_x2 = sb("scales_x2", [P, 3])
        neg_s2 = sb("neg_s2", [P, 1])
        credit = sb("credit", [P, 3])
        inh_mul = sb("inh_mul", [P, 1])
        inh_add = sb("inh_add", [P, 1])

        probs = (prob_even, prob_odd)
        x_sb = prob_odd[:, :, :].rearrange("p h (a e) -> p (h a) e", e=E)
        spare = prob_even[:, :, :].rearrange("p h s -> p (h s)").rearrange("p (n e) -> p n e", e=E)
        H_RING, E_RING = 4, 2
        h_full = spare[:, 0:H_RING, :]
        e_buf = spare[:, H_RING:H_RING + E_RING, :]
        ffn_w = (w_hi[:, 0:CHUNKS, :, :].rearrange("p n c d -> p n (c d)"),
                 w_lo[:, 0:CHUNKS, :, :].rearrange("p n c d -> p n (c d)"), wd_hi)
        ffn_in = ((xn_hi, xn_lo), (q_hi, q_lo), (xn_hi, xn_lo))

        ps_s = ps("ps_s", [P, SCORE_RING, S])
        ps_t = [ps(f"ps_t{n}", [P, HEADS, P]) for n in range(TURN_RING)]
        ps_o = ps("ps_o", [P, HEADS * P])
        ps_m = ps("ps_m", [P, E])
        banks4 = ps_s[:, :, :].rearrange("p r (a e) -> p (r a) e", e=E)
        BANKS4 = 4

        x_loaded = [sem(f"x_loaded{b}") for b in range(BLOCKS)]
        scales_loaded = sem("scales_loaded")
        raw_loaded = [sem(f"raw_loaded{n}") for n in range(RAW)]
        x_again = sem("x_again")
        stored = sem("stored")
        consts = sem("consts")
        ln_step = sem("ln_step")
        ln_sqrt = sem("ln_sqrt")
        ln_turned = sem("ln_turned")
        ln_hi = sem("ln_hi")
        ln_lo = sem("ln_lo")
        xn_ready = sem("xn_ready")
        w_hi_done = sem("w_hi_done")
        w_split = sem("w_split")
        shared_done = sem("shared_done")
        shared_hi = sem("shared_hi")
        shared_read = sem("shared_read")
        scores_done = sem("scores_done")
        max_done = sem("max_done")
        exp_done = sem("exp_done")
        inverse_done = sem("inverse_done")
        normed = sem("normed")
        turned = sem("turned")
        turn_hi = sem("turn_hi")
        turn_split = sem("turn_split")
        weighed = sem("weighed")
        attn_hi = sem("attn_hi")
        attn_split = sem("attn_split")
        ffn_w_built = sem("ffn_w_built")
        ffn_done = sem("ffn_done")
        ffn_act = sem("ffn_act")
        ffn_full = sem("ffn_full")
        ffn_lo = sem("ffn_lo")
        scaled = sem("scaled")
        fin_step = sem("fin_step")
        row_ready = sem("row_ready")

        LN_STEPS = 2 * BLOCKS + 1
        ATTN_SHARED = PRO_SHARED + BODY_SHARED * (GROUPS - 1) + len(shared(LAST))
        K_PIECE = PRO_PIECES + BODY_PIECES * (GROUPS - 1) + HEADS
        FFN_UNITS = CHUNKS * 2

        def ffn_units():
            return [(layer, half, o) for layer in range(2) for half in range(2)
                    for o in range(CHUNKS)]

        block = ctx.enter_context(nc.Block())

        @block.sync
        def _(sp):
            for b in range(BLOCKS):
                sp.dma_start(x_sb[:, b, :], x_d[b * P:(b + 1) * P, :]).then_inc(x_loaded[b], 16)

            def load(items, g):
                pro = items is PROLOGUE
                run = Runs(items, g)
                for n, piece in enumerate(run.splits):
                    if not pro or n >= RAW:
                        sp.wait_ge(w_split, run.piece0 + n + 1 - RAW)
                    slot = raw_slot(pro, n)
                    if piece.startswith("wd"):
                        src = wd_d[bass.ds(g, 1), int(piece[2]), :, :]
                    else:
                        src = wqkv_d[bass.ds(g + 1, 1), PIECES.index(piece), :, :]
                    sp.dma_start(raw[:, slot, :], src.rearrange("a p e -> (a p) e"))\
                      .then_inc(raw_loaded[slot], 16)

            for n, s_d in enumerate(s_ds):
                sp.dma_start(scales[:, n:n + 1], s_d.partition_broadcast(P)).then_inc(scales_loaded, 16)
            load(PROLOGUE, -1)
            with sp.Fori(0, GROUPS - 1) as g:
                load(BODY, g)
            load(LAST, GROUPS - 1)
            for n, k_d in enumerate(k_ds):
                sp.wait_ge(w_split, K_PIECE + n + 1 - RAW)
                slot = (K_PIECE + n) % RAW
                sp.dma_start(raw[:, slot, :].bitcast(U8).rearrange("p (c o) -> p c o", o=E),
                             k_d.rearrange("(c p) o -> p c o", p=P)).then_inc(raw_loaded[slot], 16)
            sp.wait_ge(turned, TURNS * GROUPS)
            sp.dma_start(x_sb, x_d.rearrange("(b p) e -> p b e", p=P)).then_inc(x_again, 16)
            for b in range(BLOCKS):
                sp.wait_ge(row_ready, b + 1)
                sp.dma_start(out_d[b * P:(b + 1) * P, :], y[:, b, :]).then_inc(stored, 16)
            sp.wait_ge(stored, 16 * BLOCKS)

        @block.gpsimd
        def _(pool):
            pool.memset(ident[:, :], 0.0).then_inc(consts, 1)
            pool.memset(ident_b[:, :], 0.0).then_inc(consts, 1)
            pool.memset(mask_b[:, :], 0.0).then_inc(consts, 1)
            pool.memset(inh_mul[:, :], 2.0).then_inc(consts, 1)
            pool.memset(inh_add[:, :], -1.0).then_inc(consts, 1)
            pool.wait_ge(consts, 5)
            for m in (ident, ident_b):
                pool.affine_select(out=m[:, :], in_=m[:, :], compare_op=ALU.not_equal, fill=1.0,
                                   base=0, pattern=[[-1, P]], channel_multiplier=1).then_inc(consts, 1)
            pool.affine_select(out=mask_b[:, :], in_=mask_b[:, :], compare_op=ALU.is_ge, fill=MASKED,
                               base=0, pattern=[[-1, P]], channel_multiplier=1).then_inc(consts, 1)
            first = EXC - (CHUNKS - 1) * P
            for m, v in ((inh_mul, 2.0 * INH_FACTOR), (inh_add, -INH_FACTOR)):
                pool.affine_select(out=m[:, :], in_=m[:, :], compare_op=ALU.is_ge, fill=v,
                                   base=first - 1, pattern=[[0, 1]], channel_multiplier=-1)\
                    .then_inc(consts, 1)
            pool.memset(y[:, :, :], 0.0).then_inc(consts, 1)

            def run(items, g):
                r = Runs(items, g)
                for item in items:
                    if item[0] == "scores":
                        _, i, h = item
                        n = SCORES * r.group_of_scores(i) + HEADS * i + h
                        slot = (HEADS * i + h) % STAT_RING
                        rows = probs[i % 2][:, h, 0:(i + 1) * P]
                        pool.wait_ge(inverse_done, n + 1)
                        pool.tensor_tensor(rows, rows, row_inv[:, slot:slot + 1]
                                           .to_broadcast([P, (i + 1) * P]), ALU.mult)\
                            .then_inc(normed, 1)

            run(PROLOGUE, -1)
            with pool.Fori(0, GROUPS - 1) as g:
                run(BODY, g)
            run(LAST, GROUPS - 1)

            for u, (layer, half, o) in enumerate(ffn_units()):
                hi, lo = ffn_in[layer + 1]
                pool.wait_ge(ffn_full, u + 1)
                pool.tensor_tensor(lo[:, o, half * HALF:(half + 1) * HALF], h_full[:, u % H_RING, :],
                                   hi[:, o, half * HALF:(half + 1) * HALF], ALU.subtract)\
                    .then_inc(ffn_lo, 1)
            pool.wait_ge(x_again, 16)
            for b in range(BLOCKS):
                pool.wait_ge(fin_step, 4 * b + 4)
                pool.tensor_tensor(y[:, b, :], y[:, b, :], x_sb[:, b, :], ALU.add).then_inc(row_ready, 1)

        @block.scalar
        def _(act):
            act.wait_ge(ln_step, LN_STEPS)
            act.activation(std[:, :], var_eps[:, :], ACT.Sqrt).then_inc(ln_sqrt, 1)
            act.wait_ge(ln_sqrt, 1)
            act.activation(credit[:, 0:1], std[:, 0:1], ACT.Copy).then_inc(exp_done, SCORE_RING)

            def turn_xn(b):
                act.wait_ge(ln_turned, b + 1)
                act.activation(xn_hi[:, :, b * P:(b + 1) * P],
                               banks4[:, b % BANKS4, :].rearrange("p (c t) -> p c t", t=P),
                               ACT.Copy).then_inc(ln_hi, 1)

            def run(items, g):
                r = Runs(items, g)
                pro = items is PROLOGUE
                for item in items:
                    kind = item[0]
                    if kind == "scores":
                        _, i, h = item
                        n = SCORES * r.group_of_scores(i) + HEADS * i + h
                        slot = (HEADS * i + h) % STAT_RING
                        act.wait_ge(max_done, n + 1)
                        act.activation(probs[i % 2][:, h, 0:(i + 1) * P],
                                       ps_s[:, h % SCORE_RING, 0:(i + 1) * P],
                                       ACT.Exp, bias=neg_max[:, slot:slot + 1],
                                       accum_out=row_sum[:, slot:slot + 1]).then_inc(exp_done, 1)
                    elif kind == "turn":
                        _, i, j = item
                        t = tri(i) + j
                        act.wait_ge(turned, TURNS * g + t + 1)
                        act.activation(pt_hi[:, t % PT_RING, :, :], ps_t[t % TURN_RING][:, :, :],
                                       ACT.Copy).then_inc(turn_hi, 1)
                    elif kind == "weigh" and item[1] == item[2]:
                        i = item[1]
                        act.wait_ge(weighed, BLOCKS * g + i + 1)
                        act.activation(at_hi[:, i % ATTN_RING, :, :],
                                       ps_o[:, :].rearrange("p (h t) -> p h t", t=P),
                                       ACT.Copy).then_inc(attn_hi, 1)
                    elif kind == "unit" and item[1] != "v":
                        _, piece, half = item
                        act.wait_ge(shared_done, r.shared_no(item))
                        cols = slice(half * HALF, (half + 1) * HALF)
                        if piece == "k":
                            act.activation(k_hi[:, cols], ps_m[:, :], ACT.Copy).then_inc(shared_hi, 1)
                        else:
                            act.activation(q_hi[:, int(piece[1]), cols], ps_m[:, :], ACT.Copy,
                                           scale=SCALE).then_inc(shared_hi, 1)
                    elif kind == "vblocks":
                        half = item[1]
                        act.wait_ge(shared_done, r.shared_no(item))
                        act.activation(v_hi[:, half * 4:half * 4 + 4, :],
                                       ps_m[:, :].rearrange("p (b d) -> p b d", d=P),
                                       ACT.Copy).then_inc(shared_hi, 1)
                    elif kind == "split":
                        piece = item[1]
                        n = r.splits.index(piece)
                        slot = raw_slot(pro, n)
                        act.wait_ge(raw_loaded[slot], 16 * raw_turn(pro, n, g))
                        if piece.startswith("wd"):
                            act.wait_ge(shared_done, r.shared0)
                            dst = wd_hi[:, int(piece[2]), :]
                        else:
                            if not pro:
                                act.wait_ge(shared_done, r.shared_no(("unit", piece, 1)))
                            dst = w_hi[:, PIECES.index(piece), :, :].rearrange("p c d -> p (c d)")
                        act.activation(dst, raw[:, slot, :], ACT.Copy).then_inc(w_hi_done, 1)

            for b in range(BLOCKS):
                turn_xn(b)
            run(PROLOGUE, -1)
            with act.Fori(0, GROUPS - 1) as g:
                run(BODY, g)
            run(LAST, GROUPS - 1)

            act.wait_ge(scaled, 2)
            for u, (layer, half, o) in enumerate(ffn_units()):
                hi, _ = ffn_in[layer + 1]
                act.wait_ge(ffn_done, u + 1)
                act.activation(hi[:, o, half * HALF:(half + 1) * HALF], banks4[:, u % BANKS4, :],
                               ACT.Relu, scale=scales_x2[:, layer:layer + 1]).then_inc(ffn_act, 1)
            for b in range(BLOCKS):
                u = 2 * FFN_UNITS + b
                act.wait_ge(ffn_done, u + 1)
                if b >= E_RING:
                    act.wait_ge(fin_step, 4 * (b - E_RING) + 4)
                act.activation(e_buf[:, b % E_RING, :], banks4[:, u % BANKS4, :], ACT.Exp,
                               scale=neg_s2[:, 0:1]).then_inc(ffn_act, 1)

        @block.vector
        def _(dve):
            for b in range(BLOCKS):
                dve.wait_ge(x_loaded[b], 16)
                dve.bn_stats(bn[:, b, :], x_sb[:, b, :]).then_inc(ln_step, 1)
            for b in range(BLOCKS):
                dve.wait_ge(ln_step, b + 1)
                dve.bn_aggr(mv[:, b, :], bn[:, b, :]).then_inc(ln_step, 1)
            dve.wait_ge(ln_step, 2 * BLOCKS)
            dve.tensor_scalar(var_eps[:, :], mv[:, :, 1], EPS, None, ALU.add).then_inc(ln_step, 1)
            dve.wait_ge(ln_sqrt, 1)
            dve.reciprocal(rstd[:, :], std[:, :]).then_inc(ln_step, 1)
            dve.wait_ge(ln_step, LN_STEPS + 1)
            dve.tensor_tensor(newton[:, :], rstd[:, :], rstd[:, :], ALU.mult).then_inc(ln_step, 1)
            dve.wait_ge(ln_step, LN_STEPS + 2)
            dve.tensor_tensor(newton[:, :], newton[:, :], var_eps[:, :], ALU.mult).then_inc(ln_step, 1)
            dve.wait_ge(ln_step, LN_STEPS + 3)
            dve.tensor_scalar(newton[:, :], newton[:, :], -0.5, 1.5, ALU.mult, ALU.add)\
                .then_inc(ln_step, 1)
            dve.wait_ge(ln_step, LN_STEPS + 4)
            dve.tensor_tensor(rstd[:, :], rstd[:, :], newton[:, :], ALU.mult).then_inc(ln_step, 1)
            dve.wait_ge(ln_step, LN_STEPS + 5)
            for b in range(BLOCKS):
                dve.tensor_scalar(x_sb[:, b, :], x_sb[:, b, :], mv[:, b, 0:1], rstd[:, b:b + 1],
                                  ALU.subtract, ALU.mult).then_inc(xn_ready, 1)
            for b in range(BLOCKS):
                dve.wait_ge(ln_hi, b + 1)
                dve.tensor_tensor(xn_lo[:, :, b * P:(b + 1) * P],
                                  banks4[:, b % BANKS4, :].rearrange("p (c t) -> p c t", t=P),
                                  xn_hi[:, :, b * P:(b + 1) * P], ALU.subtract).then_inc(ln_lo, 1)
            dve.wait_ge(scales_loaded, 16 * 3)
            dve.tensor_scalar(scales_x2[:, :], scales[:, :], 2.0, None, ALU.mult).then_inc(scaled, 1)
            dve.tensor_scalar(neg_s2[:, :], scales[:, 2:3], -1.0, None, ALU.mult).then_inc(scaled, 1)
            dve.memset(credit[:, 1:2], 0.0).then_inc(turn_split, TURN_RING)
            dve.memset(credit[:, 2:3], 0.0).then_inc(attn_split, 1)
            dve.wait_ge(consts, 11)

            def run(items, g):
                r = Runs(items, g)
                pro = items is PROLOGUE
                for item in items:
                    kind = item[0]
                    if kind == "scores":
                        _, i, h = item
                        n = SCORES * r.group_of_scores(i) + HEADS * i + h
                        slot = (HEADS * i + h) % STAT_RING
                        dve.wait_ge(scores_done, n + 1)
                        dve.tensor_reduce(neg_max[:, slot:slot + 1],
                                          ps_s[:, h % SCORE_RING, 0:(i + 1) * P], AX_X, ALU.max,
                                          negate=True).then_inc(max_done, 1)
                    elif kind == "inverse":
                        _, i, h = item
                        n = SCORES * r.group_of_scores(i) + HEADS * i + h
                        slot = (HEADS * i + h) % STAT_RING
                        dve.wait_ge(exp_done, n + 1 + SCORE_RING)
                        dve.reciprocal(row_inv[:, slot:slot + 1], row_sum[:, slot:slot + 1])\
                            .then_inc(inverse_done, 1)
                    elif kind == "turn":
                        _, i, j = item
                        t = tri(i) + j
                        dve.wait_ge(turn_hi, TURNS * g + t + 1)
                        dve.tensor_tensor(pt_lo[:, t % PT_RING, :, :], ps_t[t % TURN_RING][:, :, :],
                                          pt_hi[:, t % PT_RING, :, :], ALU.subtract)\
                            .then_inc(turn_split, 1)
                    elif kind == "weigh" and item[1] == item[2]:
                        i = item[1]
                        dve.wait_ge(attn_hi, BLOCKS * g + i + 1)
                        dve.tensor_tensor(at_lo[:, i % ATTN_RING, :, :],
                                          ps_o[:, :].rearrange("p (h t) -> p h t", t=P),
                                          at_hi[:, i % ATTN_RING, :, :], ALU.subtract)\
                            .then_inc(attn_split, 1)
                    elif kind == "unit":
                        _, piece, half = item
                        cols = slice(half * HALF, (half + 1) * HALF)
                        if piece == "v":
                            dve.wait_ge(shared_done, r.shared_no(item))
                            dve.tensor_copy(vt[:, cols], ps_m[:, :]).then_inc(shared_read, 1)
                            continue
                        dve.wait_ge(shared_hi, r.hi_no(item))
                        if piece == "k":
                            dve.tensor_tensor(k_lo[:, cols], ps_m[:, :], k_hi[:, cols],
                                              ALU.subtract).then_inc(shared_read, 1)
                        else:
                            h = int(piece[1])
                            dve.scalar_tensor_tensor(out=q_lo[:, h, cols], in0=ps_m[:, :],
                                                     scalar=SCALE, in1=q_hi[:, h, cols],
                                                     op0=ALU.mult, op1=ALU.subtract)\
                                .then_inc(shared_read, 1)
                    elif kind == "vblocks":
                        half = item[1]
                        dve.wait_ge(shared_hi, r.hi_no(item))
                        dve.tensor_tensor(v_lo[:, half * 4:half * 4 + 4, :],
                                          ps_m[:, :].rearrange("p (b d) -> p b d", d=P),
                                          v_hi[:, half * 4:half * 4 + 4, :], ALU.subtract)\
                            .then_inc(shared_read, 1)
                    elif kind == "dense":
                        i = item[1]
                        dve.wait_ge(shared_done, r.shared_no(item))
                        dve.wait_ge(shared_read, r.shared_no(item) - 1)
                        dve.tensor_tensor(y[:, i, :], ps_m[:, :], y[:, i, :], ALU.add)\
                            .then_inc(shared_read, 1)
                    elif kind == "split":
                        piece = item[1]
                        slot = raw_slot(pro, r.splits.index(piece))
                        dve.wait_ge(w_hi_done, r.piece_no(piece))
                        if piece.startswith("wd"):
                            hi, lo = (w[:, int(piece[2]), :] for w in (wd_hi, wd_lo))
                        else:
                            hi, lo = (w[:, PIECES.index(piece), :, :].rearrange("p c d -> p (c d)")
                                      for w in (w_hi, w_lo))
                        dve.tensor_tensor(lo, raw[:, slot, :], hi, ALU.subtract).then_inc(w_split, 1)

            run(PROLOGUE, -1)
            with dve.Fori(0, GROUPS - 1) as g:
                run(BODY, g)
            run(LAST, GROUPS - 1)

            for layer in range(3):
                slot = (K_PIECE + layer) % RAW
                bits = raw[:, slot, :].bitcast(U8).rearrange("p (c o) -> p c o", o=E)
                dve.wait_ge(raw_loaded[slot], 16 * ((K_PIECE + layer) // RAW + 1))
                dve.wait_ge(shared_done, ATTN_SHARED)
                whole = CHUNKS if layer == 0 else CHUNKS - 1
                dve.tensor_scalar(ffn_w[layer][:, 0:whole, :], bits[:, 0:whole, :], 2.0, -1.0,
                                  ALU.mult, ALU.add).then_inc(ffn_w_built, 1)
                if layer:
                    dve.tensor_scalar(ffn_w[layer][:, whole, :], bits[:, whole, :], inh_mul[:, 0:1],
                                      inh_add[:, 0:1], ALU.mult, ALU.add).then_inc(ffn_w_built, 1)
            for u, (layer, half, o) in enumerate(ffn_units()):
                dve.wait_ge(ffn_act, u + 1)
                if u >= H_RING:
                    dve.wait_ge(ffn_lo, u + 1 - H_RING)
                else:
                    dve.wait_ge(normed, SCORES * GROUPS)
                    dve.wait_ge(turned, TURNS * GROUPS)
                dve.tensor_scalar(h_full[:, u % H_RING, :], banks4[:, u % BANKS4, :],
                                  scales_x2[:, layer:layer + 1], 0.0, ALU.mult, ALU.max)\
                    .then_inc(ffn_full, 1)
            for b in range(BLOCKS):
                u = 2 * FFN_UNITS + b
                eb = e_buf[:, b % E_RING, :]
                dve.wait_ge(ffn_act, u + 1)
                dve.scalar_tensor_tensor(out=y[:, b, :], in0=banks4[:, u % BANKS4, :],
                                         scalar=scales[:, 2:3], in1=y[:, b, :],
                                         op0=ALU.mult, op1=ALU.mult).then_inc(fin_step, 1)
                dve.tensor_scalar(eb, eb, 1.0, None, ALU.add).then_inc(fin_step, 1)
                dve.wait_ge(fin_step, 4 * b + 2)
                dve.reciprocal(eb, eb).then_inc(fin_step, 1)
                dve.wait_ge(fin_step, 4 * b + 3)
                dve.tensor_tensor(y[:, b, :], y[:, b, :], eb, ALU.mult).then_inc(fin_step, 1)

        @block.tensor
        def _(pe):
            def three(out, sta, mov, start, stop):
                (sta_hi, sta_lo), (mov_hi, mov_lo) = sta, mov
                pe.matmul(out, sta_hi, mov_hi, start=start, stop=False)
                pe.matmul(out, sta_hi, mov_lo, start=False, stop=False)
                return pe.matmul(out, sta_lo, mov_hi, start=False, stop=stop)

            pe.wait_ge(consts, 10)
            for b in range(BLOCKS):
                pe.wait_ge(xn_ready, b + 1)
                if b >= BANKS4:
                    pe.wait_ge(ln_lo, b + 1 - BANKS4)
                for c in range(CHUNKS):
                    mm = pe.transpose(banks4[:, b % BANKS4, c * P:(c + 1) * P],
                                      x_sb[:, b, c * P:(c + 1) * P], ident[:, :])
                mm.then_inc(ln_turned, 1)
            pe.wait_ge(ln_lo, BLOCKS)

            def run(items, g):
                r = Runs(items, g)
                pro = items is PROLOGUE
                for item in items:
                    kind = item[0]
                    if kind == "scores":
                        _, i, h = item
                        n = SCORES * r.group_of_scores(i) + HEADS * i + h
                        if i in (0, 4):
                            half = i // 4
                            pe.wait_ge(shared_read, r.shared0 + 1 + max(
                                r.order.index(("unit", p, half)) for p in (f"q{h}", "k")))
                        pe.wait_ge(exp_done, n + 1)
                        rows = slice(i * P, (i + 1) * P)
                        sta = q_hi[:, h, rows], q_lo[:, h, rows]
                        width = (i + 1) * P
                        buf = ps_s[:, h % SCORE_RING, :]
                        for at in range(0, width, E):
                            cols = slice(at, min(at + E, width))
                            diag = at + E >= width
                            three(buf[:, cols], sta, (k_hi[:, cols], k_lo[:, cols]), True, not diag)
                        pe.matmul(buf[:, rows], ident_b[:, :], mask_b[:, :], start=False, stop=True)\
                            .then_inc(scores_done, 1)
                    elif kind == "turn":
                        _, i, j = item
                        t = tri(i) + j
                        pe.wait_ge(turn_split, TURNS * g + t + 1)
                        if j == 0:
                            pe.wait_ge(normed, SCORES * g + HEADS * (i + 1))
                        for h in range(HEADS):
                            mm = pe.transpose(ps_t[t % TURN_RING][:, h, :],
                                              probs[i % 2][:, h, j * P:(j + 1) * P], ident[:, :])
                        mm.then_inc(turned, 1)
                    elif kind == "weigh":
                        _, i, j = item
                        t = tri(i) + j
                        if (i, j) in ((0, 0), (4, 4)):
                            before = r.shared0 if j == 0 else r.shared_no(("vblocks", 1))
                            pe.wait_ge(shared_read, before)
                        if j == 0:
                            pe.wait_ge(attn_split, BLOCKS * g + i + 1)
                        pe.wait_ge(turn_split, TURNS * g + t + 1 + TURN_RING)
                        mm = three(ps_o[:, :], (v_hi[:, j, :], v_lo[:, j, :]),
                                   tuple(pt[:, t % PT_RING, :, :].rearrange("p h t -> p (h t)")
                                         for pt in (pt_hi, pt_lo)), j == 0, j == i)
                        if j == i:
                            mm.then_inc(weighed, 1)
                    elif kind == "unit":
                        _, piece, half = item
                        no = r.shared_no(item)
                        if not pro or item != r.order[0]:
                            pe.wait_ge(shared_read, no - 1)
                        if half == 0:
                            pe.wait_ge(w_split, r.piece_no(piece))
                        cols = slice(half * HALF, (half + 1) * HALF)
                        w = PIECES.index(piece)
                        for c in range(CHUNKS):
                            mm = three(ps_m[:, :], (w_hi[:, w, c, :], w_lo[:, w, c, :]),
                                       (xn_hi[:, c, cols], xn_lo[:, c, cols]), c == 0, c == CHUNKS - 1)
                        mm.then_inc(shared_done, 1)
                    elif kind == "vblocks":
                        half = item[1]
                        pe.wait_ge(shared_read, r.shared_no(item) - 1)
                        for n in range(4):
                            b = half * 4 + n
                            mm = pe.transpose(ps_m[:, n * P:(n + 1) * P], vt[:, b * P:(b + 1) * P],
                                              ident[:, :])
                        mm.then_inc(shared_done, 1)
                    elif kind == "dense":
                        i = item[1]
                        pe.wait_ge(shared_read, r.shared_no(item) - 1)
                        pe.wait_ge(attn_split, BLOCKS * g + i + 2)
                        if i == 0:
                            pe.wait_ge(w_split, r.piece_no(f"wd{HEADS - 1}"))
                        for h in range(HEADS):
                            mm = three(ps_m[:, :], (at_hi[:, i % ATTN_RING, h, :],
                                                    at_lo[:, i % ATTN_RING, h, :]),
                                       (wd_hi[:, h, :], wd_lo[:, h, :]), h == 0, h == HEADS - 1)
                        mm.then_inc(shared_done, 1)

            run(PROLOGUE, -1)
            with pe.Fori(0, GROUPS - 1) as g:
                run(BODY, g)
            run(LAST, GROUPS - 1)

            pe.wait_ge(exp_done, SCORES * GROUPS + SCORE_RING)
            for u, (layer, half, o) in enumerate(ffn_units()):
                pe.wait_ge(ffn_w_built, 1 if layer == 0 else 3)
                if u >= BANKS4:
                    pe.wait_ge(ffn_full, u + 1 - BANKS4)
                if layer:
                    pe.wait_ge(ffn_lo, CHUNKS * (half + 1))
                cols = slice(half * HALF, (half + 1) * HALF)
                for c in range(CHUNKS):
                    for part in (0, 1):
                        mm = pe.matmul(banks4[:, u % BANKS4, :],
                                       ffn_w[layer][:, c, o * P:(o + 1) * P],
                                       ffn_in[layer][part][:, c, cols],
                                       start=(c == 0 and part == 0), stop=(c == CHUNKS - 1 and part == 1))
                mm.then_inc(ffn_done, 1)
            pe.wait_ge(ffn_w_built, 5)
            for b in range(BLOCKS):
                u = 2 * FFN_UNITS + b
                if b < BANKS4:
                    pe.wait_ge(ffn_full, u + 1 - BANKS4)
                else:
                    pe.wait_ge(fin_step, 4 * (b - BANKS4) + 1)
                pe.wait_ge(ffn_lo, FFN_UNITS + CHUNKS * (b // 4 + 1))
                for c in range(CHUNKS):
                    for part in (0, 1):
                        mm = pe.matmul(banks4[:, u % BANKS4, :],
                                       ffn_in[2][part][:, c, b * P:(b + 1) * P],
                                       ffn_w[2][:, c, :],
                                       start=(c == 0 and part == 0), stop=(c == CHUNKS - 1 and part == 1))
                mm.then_inc(ffn_done, 1)


def kernel(**inputs):
    import numpy as np
    import concourse.bacc as bacc
    from concourse.bass_utils import run_bass_kernel_spmd

    x = np.ascontiguousarray(inputs["L0_attn_q"]).reshape(S, E)
    w = np.asarray(inputs["L0_attn_w_qkv"])
    wq = w[:GROUPS * HEADS * P].reshape(GROUPS, HEADS, P, CHUNKS, P)
    wk = w[GROUPS * HEADS * P:][:GROUPS * P].reshape(GROUPS, 1, P, CHUNKS, P)
    wv = w[(GROUPS * HEADS + GROUPS) * P:].reshape(GROUPS, 1, P, CHUNKS, P)
    wqkv = np.ascontiguousarray(np.concatenate([wq, wv, wk], 1).transpose(0, 1, 4, 3, 2))
    wqkv = wqkv.reshape(GROUPS, PRO_PIECES, P, E)
    wd = np.ascontiguousarray(np.asarray(inputs["L0_attn_w_dense"]).T).reshape(GROUPS, HEADS, P, E)
    arrays = {"x": x, "wqkv": wqkv, "wd": wd}
    for n in range(3):
        arrays[f"k{n}"] = np.ascontiguousarray(inputs[f"L0_ffn_k{n}"])
        arrays[f"s{n}"] = np.asarray(inputs[f"L0_ffn_s{n}"]).reshape(1)

    nc = bacc.Bacc("TRN2", target_bir_lowering=False, num_devices=1)
    ap = {name: nc.dram_tensor(name, a.shape, mybir.dt.from_np(a.dtype), kind="ExternalInput").ap()
          for name, a in arrays.items()}
    out = nc.dram_tensor("out", (S, E), F32, kind="ExternalOutput").ap()
    build(nc, ap["x"], ap["wqkv"], ap["wd"], [ap[f"k{n}"] for n in range(3)],
          [ap[f"s{n}"] for n in range(3)], out)
    result = run_bass_kernel_spmd(nc, [arrays], core_ids=[0]).results[0]["out"]
    return result.reshape(1, S, E)
```

```python
from contextlib import ExitStack

import concourse.bass as bass
from concourse import mybir

F32 = mybir.dt.float32
F32R = mybir.dt.float32r
BF16 = mybir.dt.bfloat16
U8 = mybir.dt.uint8
ACT = mybir.ActivationFunctionType
ALU = mybir.AluOpType
AX_X = mybir.AxisListType.X

P = 128
S, E = 1024, 512
GROUPS, HEADS = 8, 4
BLOCKS = S // P
CHUNKS = E // P
HALF = S // 2
EPS = 1e-5
SCALE = float(P) ** -0.5
MASKED = -1e37
EXC = round(E * 0.8)
INH_FACTOR = -0.8 / (1.0 - 0.8)

RAW = 5
TURN_RING = 2
PT_RING = 4
ATTN_RING = 2
STAT_RING = 8

PIECES = ["q0", "q1", "q2", "q3", "v", "k"]
PRO_PIECES = len(PIECES)
BODY_PIECES = HEADS + PRO_PIECES


def tri(i):
    return i * (i + 1) // 2


TURNS = tri(BLOCKS)
SCORES = HEADS * BLOCKS


BUSY = 1e9
PASS, SHORT_PASS, SIGNAL = 0.216, 0.109, 0.21


def columns_cost(width):
    return 3 * sum(max(SHORT_PASS, PASS * min(E, width - at) / E) for at in range(0, width, E))


def pe_queues(kind):
    pro, last = kind == "prologue", kind == "last"
    unit = lambda piece, half: [("unit", piece, half, c) for c in range(CHUNKS)]
    nxt = sum((unit(p, 0) for p in PIECES), []) + [("vblocks", 0)]
    first_scores = [("scores", 0, h) for h in range(HEADS)]
    if pro:
        return [first_scores, [], [], nxt, [], []]
    turns, weighs = ([(name, i, j) for i in range(BLOCKS) for j in range(i + 1)]
                     for name in ("turn", "weigh"))
    scores = [("scores", i, h) for i in range(1, BLOCKS) for h in range(HEADS)]
    units = sum((unit(p, 1) for p in ("q0", "k", "q1", "q2", "q3", "v")), []) + [("vblocks", 1)]
    dense = [("dense", i, h) for i in range(BLOCKS) for h in range(HEADS)]
    hidden = [("hidden", layer, half, o, c) for half in range(2) for layer in range(2)
              for o in range(CHUNKS) for c in range(CHUNKS)]
    if last:
        return [scores, turns, weighs, units, dense, hidden]
    return [scores + first_scores, turns, weighs, units + nxt, dense, []]


def pe_cost(item):
    kind = item[0]
    if kind == "scores":
        return columns_cost((item[1] + 1) * P) + SHORT_PASS / 2
    if kind in ("turn", "vblocks"):
        return 4 * SHORT_PASS
    return PASS * (2 if kind == "hidden" else 3)


def whole(item):
    return item[:-1] if item[0] in ("unit", "dense", "hidden") else item


def plan(kind, leads):
    queues = pe_queues(kind)
    total = [sum(map(pe_cost, q)) or 1 for q in queues]
    done, at = [0.0] * len(queues), [0] * len(queues)
    orders = {"pe": [], "act": [], "dve": [], "pool": []}
    free = {"act": 0.0, "dve": 0.0, "pool": 0.0}
    tasks = []
    there = {}
    end = {}
    bank = {}
    t, number, open_item = 0.0, 0, None

    def task(at_time, engine, name, duration, then):
        nonlocal number
        number += 1
        tasks.append((at_time + SIGNAL, number, engine, name, duration, then))

    def chain(at_time, steps, then):
        engine, name, duration = steps[0]
        rest = steps[1:]
        task(at_time, engine, name, duration,
             (lambda e: chain(e, rest, then)) if rest else (lambda e: then(e + SIGNAL)))

    def advance(until):
        while tasks:
            best = min(tasks, key=lambda x: (max(free[x[2]], x[0]), x[0], x[1]))
            start = max(free[best[2]], best[0])
            if start > until:
                return
            tasks.remove(best)
            free[best[2]] = start + best[4]
            orders[best[2]].append(best[3])
            best[5](start + best[4])

    def free_bank(*names):
        return lambda e: bank.update({n: e for n in names})

    def ready(item):
        what = item[0]
        if what == "scores":
            i, h = item[1:]
            half = i // 4
            if i in (0, 4):
                for p in ("k", f"q{h}"):
                    if ("unit", p, half) not in there:
                        return None
            if kind != "prologue" and ("turn", (i - 2) % BLOCKS, (i - 2) % BLOCKS) not in end \
                    and i != 1:
                return None
            return max([bank.get(("score", b), 0.0) for b in score_banks(i, h)]
                       + [there[("unit", p, half)] for p in ("k", f"q{h}") if i in (0, 4)])
        if what == "turn":
            i, j = item[1:]
            if i and ("norm", i, HEADS - 1) not in there:
                return None
            n = tri(i) + j
            if n >= PT_RING and ("weigh", *pairs[n - PT_RING]) not in end:
                return None
            return max(bank.get(("turn", n % 2), 0.0), there.get(("norm", i, HEADS - 1), 0.0))
        if what == "weigh":
            i, j = item[1:]
            if item not in there or ((i, j) == (4, 4) and ("vblocks", 1) not in there):
                return None
            if i == j and i >= ATTN_RING and ("dense", i - ATTN_RING, HEADS - 1) not in end:
                return None
            return max(there[item], bank.get("attn", 0.0) if j == 0 else 0.0,
                       there[("vblocks", 1)] if (i, j) == (4, 4) else 0.0)
        if open_item is not None:
            return 0.0 if open_item == whole(item) else None
        needs = []
        if what == "dense":
            needs = [("attn", item[1])] + ([("split", f"wd{HEADS - 1}")] if item[1] == 0 else [])
        elif what == "vblocks":
            needs = [("unit", "v", item[1])]
            if item[1] == 0 and kind != "prologue" and ("weigh", BLOCKS - 1, 3) not in end:
                return None
        elif what == "unit" and item[2] == 0:
            needs = [("split", item[1])]
            if kind != "prologue" and ("scores", 7 if item[1] == "k" else 3, HEADS - 1) not in end:
                return None
        elif what == "hidden":
            _, layer, half, o, c = item
            needs = [("built", layer)]
            if layer == 0 and ("scores", 4 * half + 3, HEADS - 1) not in end:
                return None
            if layer == 1:
                needs += [("hidden", 0, half, n) for n in range(CHUNKS)]
        if any(n not in there for n in needs):
            return None
        return max([bank.get("shared", 0.0)] + [there[n] for n in needs])

    pairs = [(i, j) for i in range(BLOCKS) for j in range(i + 1)]
    splits = ([] if kind == "prologue" else [f"wd{n}" for n in range(HEADS)]) \
        + ([] if kind == "last" else PIECES)
    last_split = -9.0
    while any(at[q] < len(queue) for q, queue in enumerate(queues)):
        advance(t)
        if splits and t - last_split > 2.0:
            piece = splits[0]
            if kind == "prologue" or piece.startswith("wd") \
                    or end.get(("unit", piece, 1, CHUNKS - 1), 1e9) < t:
                splits.pop(0)
                last_split = t
                chain(t, [("act", ("hi", ("split", piece)), 0.62), ("dve", ("lo", ("split", piece)), 0.6)],
                      lambda e, p=piece: there.update({("split", p): e}))
        choice = [(q, ready(queue[at[q]])) for q, queue in enumerate(queues) if at[q] < len(queue)]
        now = [(done[q] / total[q] - leads[q], q) for q, r in choice if r is not None and r <= t]
        if not now:
            t += 0.04
            continue
        _, q = min(now)
        item = queues[q][at[q]]
        at[q] += 1
        done[q] += pe_cost(item)
        t += pe_cost(item) + 0.003
        end[item] = t
        orders["pe"].append(item)
        what = item[0]
        if what == "scores":
            i, h = item[1:]
            w = (i + 1) * P
            bank.update({("score", b): BUSY for b in score_banks(i, h)})

            def after_exp(e, i=i, h=h, w=w):
                free_bank(*[("score", b) for b in score_banks(i, h)])(e + SIGNAL)
                chain(e, [("dve", ("inverse", i, h), 0.07), ("pool", ("norm", i, h), 0.15 + w / 440)],
                      lambda e2: there.update({("norm", i, h): e2}))
            task(t, "dve", ("max", i, h), 0.125 + w / 960,
                 lambda e, i=i, h=h, w=w, f=after_exp: task(e, "act", ("exp", i, h), 0.25 + w / 1200, f))
        elif what == "turn":
            i, j = item[1:]
            bank[("turn", (tri(i) + j) % 2)] = BUSY

            def turn_split_at(e, i=i, j=j):
                bank[("turn", (tri(i) + j) % 2)] = e
                there[("weigh", i, j)] = e
            chain(t, [("act", ("hi", item), 0.48), ("dve", ("lo", item), 0.61)], turn_split_at)
        elif what == "weigh" and item[1] == item[2]:
            bank["attn"] = BUSY
            chain(t, [("act", ("hi", item), 0.48), ("dve", ("lo", item), 0.61)],
                  lambda e, i=item[1]: (bank.update({"attn": e}), there.update({("attn", i): e})))
        elif what in ("unit", "dense", "hidden", "vblocks"):
            open_item = whole(item) if what != "vblocks" and item[-1] < CHUNKS - 1 else None
            if open_item is None:
                w = whole(item)
                steps = [("act", ("hi", w), 0.48)] if has_hi(w) else []
                steps += [("dve", ("lo", w), 0.61)]
                bank["shared"] = BUSY
                if what == "hidden":
                    chain(t, steps, lambda e, w=w: (bank.update({"shared": e}), chain(
                        e, [("pool", ("low", w), 1.25)], lambda e2, w=w: there.update({w: e2}))))
                else:
                    chain(t, steps, lambda e, w=w: (bank.update({"shared": e}), there.update({w: e})))
                if w == ("hidden", 0, 1, CHUNKS - 1):
                    chain(t, [("dve", ("build", 2), 2.2)], lambda e: None)
                if kind == "last" and w == ("unit", "v", 1):
                    for layer in range(2):
                        chain(t, [("dve", ("build", layer), 2.2)],
                              lambda e, n=layer: there.update({("built", n): e}))
    for piece in splits:
        chain(t, [("act", ("hi", ("split", piece)), 0.62), ("dve", ("lo", ("split", piece)), 0.6)],
              lambda e: None)
    advance(1e9)
    return t, orders


def score_banks(i, h):
    return [h] if (i + 1) * P <= E else [2 * (h % 2), 2 * (h % 2) + 1]


def has_hi(item):
    return item[0] in ("vblocks", "hidden") or (item[0] == "unit" and item[1] != "v")


def score_exps(i, h):
    n = HEADS * i + h
    back = 1
    while not set(score_banks(i, h)) & set(score_banks((n - back) // HEADS % BLOCKS,
                                                       (n - back) % HEADS)):
        back += 1
    return n - back + 1


ORDERS = {"prologue": plan("prologue", (0, 0, 0, 0, 0, 0))[1],
          "body": plan("body", (0.05, 0.02, -0.19, 0.03, -0.25, 0))[1],
          "last": plan("last", (-0.17, -0.49, -0.52, -0.13, -0.04, -0.12))[1]}


def shared(kind):
    return [whole(i) for i in ORDERS[kind]["pe"]
            if i[0] == "vblocks" or (i[0] in ("unit", "dense", "hidden") and i[-1] == CHUNKS - 1)]


PRO_SHARED, BODY_SHARED = len(shared("prologue")), len(shared("body"))
PRO_HI = sum(map(has_hi, shared("prologue")))
BODY_HI = sum(map(has_hi, shared("body")))


class Run:

    def __init__(self, kind, g, engine):
        pro = kind == "prologue"
        self.kind, self.g, self.items = kind, g, ORDERS[kind][engine]
        self.shared0 = 0 if pro else PRO_SHARED + BODY_SHARED * g
        self.hi0 = 0 if pro else PRO_HI + BODY_HI * g
        self.piece0 = 0 if pro else PRO_PIECES + BODY_PIECES * g
        self.order = shared(kind)
        self.his = [i for i in self.order if has_hi(i)]
        self.splits = [i[1][1] for i in ORDERS[kind]["act"] if i[0] == "hi" and i[1][0] == "split"]

    def shared_no(self, item):
        return self.shared0 + self.order.index(item) + 1

    def hi_no(self, item):
        return self.hi0 + self.his.index(item) + 1

    def piece_no(self, piece):
        return self.piece0 + self.splits.index(piece) + 1

    def score_no(self, i, h):
        return SCORES * (self.g + 1 if i == 0 else self.g) + HEADS * i + h + 1

    def raw_slot(self, piece):
        n = self.splits.index(piece)
        return (n if self.kind == "prologue" else PRO_PIECES + n) % RAW

    def raw_turn(self, piece):
        n = self.splits.index(piece)
        return n // RAW + 1 if self.kind == "prologue" else \
            (PRO_PIECES + n) // RAW + 1 + BODY_PIECES // RAW * self.g


K_PIECE = PRO_PIECES + BODY_PIECES * (GROUPS - 1) + HEADS
HIDDEN = [w for w in shared("last") if w[0] == "hidden"]


def build(nc, x_d, wqkv_d, wd_d, k_ds, s_ds, out_d):
    assert BODY_PIECES % RAW == 0
    assert TURNS % TURN_RING == 0 and TURNS % PT_RING == 0
    ctx = ExitStack()
    with ctx:
        def sb(name, shape, dt=F32):
            return ctx.enter_context(nc.sbuf_tensor(name, shape, dt))

        def ps(name, shape):
            return ctx.enter_context(nc.psum_tensor(name, shape, F32))

        def sem(name):
            return ctx.enter_context(nc.semaphore(name))

        xn_hi = sb("xn_hi", [P, CHUNKS, S], F32R)
        xn_lo = sb("xn_lo", [P, CHUNKS, S], F32R)
        y = sb("y", [P, BLOCKS, E])
        raw = sb("raw", [P, RAW, E])
        w_hi = sb("w_hi", [P, PRO_PIECES, CHUNKS, P], F32R)
        w_lo = sb("w_lo", [P, PRO_PIECES, CHUNKS, P], F32R)
        wd_hi = sb("wd_hi", [P, HEADS, E], F32R)
        wd_lo = sb("wd_lo", [P, HEADS, E], F32R)
        q_hi = sb("q_hi", [P, HEADS, S], F32R)
        q_lo = sb("q_lo", [P, HEADS, S], F32R)
        k_hi = sb("k_hi", [P, S], F32R)
        k_lo = sb("k_lo", [P, S], F32R)
        vt = sb("vt", [P, S])
        v_hi = sb("v_hi", [P, BLOCKS, P], F32R)
        v_lo = sb("v_lo", [P, BLOCKS, P], F32R)
        prob_even = sb("prob_even", [P, HEADS, S - P])
        prob_odd = sb("prob_odd", [P, HEADS, S])
        pt_hi = sb("pt_hi", [P, PT_RING, HEADS, P], F32R)
        pt_lo = sb("pt_lo", [P, PT_RING, HEADS, P], F32R)
        at_hi = sb("at_hi", [P, ATTN_RING, HEADS, P], F32R)
        at_lo = sb("at_lo", [P, ATTN_RING, HEADS, P], F32R)
        ident = sb("ident", [P, P])
        ident_b = sb("ident_b", [P, P], BF16)
        mask_b = sb("mask_b", [P, P], BF16)
        neg_max = sb("neg_max", [P, STAT_RING])
        row_sum = sb("row_sum", [P, STAT_RING])
        row_inv = sb("row_inv", [P, STAT_RING])
        bn = sb("bn", [P, BLOCKS, 6])
        mv = sb("mv", [P, BLOCKS, 2])
        var_eps = sb("var_eps", [P, BLOCKS])
        std = sb("std", [P, BLOCKS])
        rstd = sb("rstd", [P, BLOCKS])
        newton = sb("newton", [P, BLOCKS])
        scales = sb("scales", [P, 3])
        scales_x2 = sb("scales_x2", [P, 3])
        neg_s2 = sb("neg_s2", [P, 1])
        credit = sb("credit", [P, 2])
        inh_mul = sb("inh_mul", [P, 1])
        inh_add = sb("inh_add", [P, 1])

        probs = (prob_even, prob_odd)
        x_sb = prob_odd[:, :, :].rearrange("p h (a e) -> p (h a) e", e=E)
        x_even = prob_even[:, :, :].rearrange("p h s -> p (h s)").rearrange("p (b e) -> p b e", e=E)
        x_back = [x_even[:, b, :] for b in range(BLOCKS - 1)] + [x_sb[:, 0, :]]
        E_RING = 2
        e_buf = x_sb[:, 1:1 + E_RING, :]
        H_SLOTS = [(K_PIECE - n) % RAW for n in (2, 1)]
        H_RING = len(H_SLOTS)
        ffn_w = [w[:, 0:CHUNKS, :, :].rearrange("p n c d -> p n (c d)") for w in (w_hi, w_lo, w_hi)]
        ffn_in = ((xn_hi, xn_lo), (q_hi, q_lo), (xn_hi, xn_lo))

        BANKS4 = 4
        ps_s = ps("ps_s", [P, BANKS4 * E])
        ps_t = [ps(f"ps_t{n}", [P, HEADS, P]) for n in range(TURN_RING)]
        ps_o = ps("ps_o", [P, HEADS * P])
        ps_m = ps("ps_m", [P, E])
        banks4 = ps_s[:, :].rearrange("p (n e) -> p n e", e=E)

        x_loaded = [sem(f"x_loaded{b}") for b in range(BLOCKS)]
        scales_loaded = sem("scales_loaded")
        raw_loaded = [sem(f"raw_loaded{n}") for n in range(RAW)]
        x_again = [sem(f"x_again{n}") for n in range(2)]
        stored = sem("stored")
        consts = sem("consts")
        ln_step = sem("ln_step")
        ln_sqrt = sem("ln_sqrt")
        ln_turned = sem("ln_turned")
        ln_hi = sem("ln_hi")
        ln_lo = sem("ln_lo")
        xn_ready = sem("xn_ready")
        w_hi_done = sem("w_hi_done")
        w_split = sem("w_split")
        shared_done = sem("shared_done")
        shared_hi = sem("shared_hi")
        shared_read = sem("shared_read")
        scores_done = sem("scores_done")
        max_done = sem("max_done")
        exp_done = sem("exp_done")
        inverse_done = sem("inverse_done")
        normed = sem("normed")
        turned = sem("turned")
        turn_hi = sem("turn_hi")
        turn_split = sem("turn_split")
        weighed = sem("weighed")
        attn_hi = sem("attn_hi")
        attn_split = sem("attn_split")
        ffn_w_built = sem("ffn_w_built")
        hidden_lo = sem("hidden_lo")
        final_done = sem("final_done")
        final_exp = sem("final_exp")
        scaled = sem("scaled")
        fin_step = sem("fin_step")
        row_ready = sem("row_ready")

        LN_STEPS = 2 * BLOCKS + 1

        block = ctx.enter_context(nc.Block())

        @block.sync
        def _(sp):
            for b in range(BLOCKS):
                sp.dma_start(x_sb[:, b, :], x_d[b * P:(b + 1) * P, :]).then_inc(x_loaded[b], 16)

            def load(kind, g):
                run = Run(kind, g, "act")
                for n, piece in enumerate(run.splits):
                    if kind != "prologue" or n >= RAW:
                        sp.wait_ge(w_split, run.piece0 + n + 1 - RAW)
                    if piece.startswith("wd"):
                        src = wd_d[bass.ds(g, 1), int(piece[2]), :, :]
                    else:
                        src = wqkv_d[bass.ds(g + 1, 1), PIECES.index(piece), :, :]
                    slot = run.raw_slot(piece)
                    sp.dma_start(raw[:, slot, :], src.rearrange("a p e -> (a p) e"))\
                      .then_inc(raw_loaded[slot], 16)

            for n, s_d in enumerate(s_ds):
                sp.dma_start(scales[:, n:n + 1], s_d.partition_broadcast(P)).then_inc(scales_loaded, 16)
            load("prologue", -1)
            with sp.Fori(0, GROUPS - 1) as g:
                load("body", g)
            load("last", GROUPS - 1)
            for n, k_d in enumerate(k_ds):
                sp.wait_ge(w_split, K_PIECE + n + 1 - RAW)
                slot = (K_PIECE + n) % RAW
                sp.dma_start(raw[:, slot, :].bitcast(U8).rearrange("p (c o) -> p c o", o=E),
                             k_d.rearrange("(c p) o -> p c o", p=P)).then_inc(raw_loaded[slot], 16)
            sp.wait_ge(turned, TURNS * GROUPS - BLOCKS)
            sp.dma_start(x_even, x_d[0:S - P, :].rearrange("(b p) e -> p b e", p=P))\
              .then_inc(x_again[0], 16)
            sp.wait_ge(turned, TURNS * GROUPS)
            sp.dma_start(x_back[BLOCKS - 1], x_d[S - P:S, :]).then_inc(x_again[1], 16)
            for b in range(BLOCKS):
                sp.wait_ge(row_ready, b + 1)
                sp.dma_start(out_d[b * P:(b + 1) * P, :], y[:, b, :]).then_inc(stored, 16)
            sp.wait_ge(stored, 16 * BLOCKS)

        @block.gpsimd
        def _(pool):
            pool.memset(ident[:, :], 0.0).then_inc(consts, 1)
            pool.memset(ident_b[:, :], 0.0).then_inc(consts, 1)
            pool.memset(mask_b[:, :], 0.0).then_inc(consts, 1)
            pool.memset(inh_mul[:, :], 2.0).then_inc(consts, 1)
            pool.memset(inh_add[:, :], -1.0).then_inc(consts, 1)
            pool.wait_ge(consts, 5)
            for m in (ident, ident_b):
                pool.affine_select(out=m[:, :], in_=m[:, :], compare_op=ALU.not_equal, fill=1.0,
                                   base=0, pattern=[[-1, P]], channel_multiplier=1).then_inc(consts, 1)
            pool.affine_select(out=mask_b[:, :], in_=mask_b[:, :], compare_op=ALU.is_ge, fill=MASKED,
                               base=0, pattern=[[-1, P]], channel_multiplier=1).then_inc(consts, 1)
            first = EXC - (CHUNKS - 1) * P
            for m, v in ((inh_mul, 2.0 * INH_FACTOR), (inh_add, -INH_FACTOR)):
                pool.affine_select(out=m[:, :], in_=m[:, :], compare_op=ALU.is_ge, fill=v,
                                   base=first - 1, pattern=[[0, 1]], channel_multiplier=-1)\
                    .then_inc(consts, 1)
            pool.memset(y[:, :, :], 0.0).then_inc(consts, 1)

            def run(kind, g):
                r = Run(kind, g, "pool")
                for what, *item in r.items:
                    if what == "norm":
                        i, h = item
                        slot = (HEADS * i + h) % STAT_RING
                        rows = probs[i % 2][:, h, 0:(i + 1) * P]
                        pool.wait_ge(inverse_done, r.score_no(i, h))
                        pool.tensor_tensor(rows, rows, row_inv[:, slot:slot + 1]
                                           .to_broadcast([P, (i + 1) * P]), ALU.mult)\
                            .then_inc(normed, 1)
                    elif what == "low":
                        _, layer, half, o = item[0]
                        hi, lo = ffn_in[layer + 1]
                        cols = slice(half * HALF, (half + 1) * HALF)
                        u = HIDDEN.index(item[0])
                        pool.wait_ge(shared_read, r.shared_no(item[0]))
                        pool.tensor_tensor(lo[:, o, cols], raw[:, H_SLOTS[u % H_RING], :],
                                           hi[:, o, cols], ALU.subtract).then_inc(hidden_lo, 1)

            run("prologue", -1)
            with pool.Fori(0, GROUPS - 1) as g:
                run("body", g)
            run("last", GROUPS - 1)

            for b in range(BLOCKS):
                if b in (0, BLOCKS - 1):
                    pool.wait_ge(x_again[b // (BLOCKS - 1)], 16)
                pool.wait_ge(fin_step, 4 * b + 4)
                pool.tensor_tensor(y[:, b, :], y[:, b, :], x_back[b], ALU.add).then_inc(row_ready, 1)

        @block.scalar
        def _(act):
            act.wait_ge(ln_step, LN_STEPS)
            act.activation(std[:, :], var_eps[:, :], ACT.Sqrt).then_inc(ln_sqrt, 1)
            def turn_xn(b):
                act.wait_ge(ln_turned, b + 1)
                act.activation(xn_hi[:, :, b * P:(b + 1) * P],
                               banks4[:, b % BANKS4, :].rearrange("p (c t) -> p c t", t=P),
                               ACT.Copy).then_inc(ln_hi, 1)

            def run(kind, g):
                r = Run(kind, g, "act")
                for what, *item in r.items:
                    if what == "exp":
                        i, h = item
                        slot = (HEADS * i + h) % STAT_RING
                        bank = score_banks(i, h)[0]
                        act.wait_ge(max_done, r.score_no(i, h))
                        act.activation(probs[i % 2][:, h, 0:(i + 1) * P],
                                       ps_s[:, bank * E:bank * E + (i + 1) * P],
                                       ACT.Exp, bias=neg_max[:, slot:slot + 1],
                                       accum_out=row_sum[:, slot:slot + 1]).then_inc(exp_done, 1)
                        continue
                    item, = item
                    name = item[0]
                    if name == "turn":
                        _, i, j = item
                        t = tri(i) + j
                        act.wait_ge(turned, TURNS * g + t + 1)
                        act.activation(pt_hi[:, t % PT_RING, :, :], ps_t[t % TURN_RING][:, :, :],
                                       ACT.Copy).then_inc(turn_hi, 1)
                    elif name == "weigh":
                        i = item[1]
                        act.wait_ge(weighed, BLOCKS * g + i + 1)
                        act.activation(at_hi[:, i % ATTN_RING, :, :],
                                       ps_o[:, :].rearrange("p (h t) -> p h t", t=P),
                                       ACT.Copy).then_inc(attn_hi, 1)
                    elif name == "unit":
                        _, piece, half = item
                        cols = slice(half * HALF, (half + 1) * HALF)
                        act.wait_ge(shared_done, r.shared_no(item))
                        if piece == "k":
                            act.activation(k_hi[:, cols], ps_m[:, :], ACT.Copy).then_inc(shared_hi, 1)
                        else:
                            act.activation(q_hi[:, int(piece[1]), cols], ps_m[:, :], ACT.Copy,
                                           scale=SCALE).then_inc(shared_hi, 1)
                    elif name == "vblocks":
                        half = item[1]
                        act.wait_ge(shared_done, r.shared_no(item))
                        act.activation(v_hi[:, half * 4:half * 4 + 4, :],
                                       ps_m[:, :].rearrange("p (b d) -> p b d", d=P),
                                       ACT.Copy).then_inc(shared_hi, 1)
                    elif name == "hidden":
                        _, layer, half, o = item
                        act.wait_ge(shared_done, r.shared_no(item))
                        act.activation(ffn_in[layer + 1][0][:, o, half * HALF:(half + 1) * HALF],
                                       ps_m[:, :], ACT.Relu, scale=scales_x2[:, layer:layer + 1])\
                            .then_inc(shared_hi, 1)
                    elif name == "split":
                        piece = item[1]
                        slot = r.raw_slot(piece)
                        act.wait_ge(raw_loaded[slot], 16 * r.raw_turn(piece))
                        if piece.startswith("wd"):
                            act.wait_ge(shared_done, r.shared0)
                            dst = wd_hi[:, int(piece[2]), :]
                        else:
                            if kind != "prologue":
                                act.wait_ge(shared_done, r.shared_no(("unit", piece, 1)))
                            dst = w_hi[:, PIECES.index(piece), :, :].rearrange("p c d -> p (c d)")
                        act.activation(dst, raw[:, slot, :], ACT.Copy).then_inc(w_hi_done, 1)

            for b in range(BLOCKS):
                turn_xn(b)
            run("prologue", -1)
            with act.Fori(0, GROUPS - 1) as g:
                run("body", g)
            act.wait_ge(scaled, 2)
            run("last", GROUPS - 1)

            for b in range(BLOCKS):
                act.wait_ge(final_done, b + 1)
                if b == 0:
                    act.wait_ge(turned, TURNS * GROUPS)
                if b >= E_RING:
                    act.wait_ge(fin_step, 4 * (b - E_RING) + 4)
                act.activation(e_buf[:, b % E_RING, :], banks4[:, b % BANKS4, :], ACT.Exp,
                               scale=neg_s2[:, 0:1]).then_inc(final_exp, 1)

        @block.vector
        def _(dve):
            for b in range(BLOCKS):
                dve.wait_ge(x_loaded[b], 16)
                dve.bn_stats(bn[:, b, :], x_sb[:, b, :]).then_inc(ln_step, 1)
            for b in range(BLOCKS):
                dve.wait_ge(ln_step, b + 1)
                dve.bn_aggr(mv[:, b, :], bn[:, b, :]).then_inc(ln_step, 1)
            dve.wait_ge(ln_step, 2 * BLOCKS)
            dve.tensor_scalar(var_eps[:, :], mv[:, :, 1], EPS, None, ALU.add).then_inc(ln_step, 1)
            dve.wait_ge(ln_sqrt, 1)
            dve.reciprocal(rstd[:, :], std[:, :]).then_inc(ln_step, 1)
            dve.wait_ge(ln_step, LN_STEPS + 1)
            dve.tensor_tensor(newton[:, :], rstd[:, :], rstd[:, :], ALU.mult).then_inc(ln_step, 1)
            dve.wait_ge(ln_step, LN_STEPS + 2)
            dve.tensor_tensor(newton[:, :], newton[:, :], var_eps[:, :], ALU.mult).then_inc(ln_step, 1)
            dve.wait_ge(ln_step, LN_STEPS + 3)
            dve.tensor_scalar(newton[:, :], newton[:, :], -0.5, 1.5, ALU.mult, ALU.add)\
                .then_inc(ln_step, 1)
            dve.wait_ge(ln_step, LN_STEPS + 4)
            dve.tensor_tensor(rstd[:, :], rstd[:, :], newton[:, :], ALU.mult).then_inc(ln_step, 1)
            dve.wait_ge(ln_step, LN_STEPS + 5)
            for b in range(BLOCKS):
                dve.tensor_scalar(x_sb[:, b, :], x_sb[:, b, :], mv[:, b, 0:1], rstd[:, b:b + 1],
                                  ALU.subtract, ALU.mult).then_inc(xn_ready, 1)
            for b in range(BLOCKS):
                dve.wait_ge(ln_hi, b + 1)
                dve.tensor_tensor(xn_lo[:, :, b * P:(b + 1) * P],
                                  banks4[:, b % BANKS4, :].rearrange("p (c t) -> p c t", t=P),
                                  xn_hi[:, :, b * P:(b + 1) * P], ALU.subtract).then_inc(ln_lo, 1)
            dve.wait_ge(scales_loaded, 16 * 3)
            dve.tensor_scalar(scales_x2[:, :], scales[:, :], 2.0, None, ALU.mult).then_inc(scaled, 1)
            dve.tensor_scalar(neg_s2[:, :], scales[:, 2:3], -1.0, None, ALU.mult).then_inc(scaled, 1)
            dve.memset(credit[:, 0:1], 0.0).then_inc(turn_split, TURN_RING)
            dve.memset(credit[:, 1:2], 0.0).then_inc(attn_split, 1)
            dve.wait_ge(consts, 11)

            def run(kind, g):
                r = Run(kind, g, "dve")
                for what, *item in r.items:
                    if what == "max":
                        i, h = item
                        slot = (HEADS * i + h) % STAT_RING
                        bank = score_banks(i, h)[0]
                        dve.wait_ge(scores_done, r.score_no(i, h))
                        dve.tensor_reduce(neg_max[:, slot:slot + 1],
                                          ps_s[:, bank * E:bank * E + (i + 1) * P], AX_X, ALU.max,
                                          negate=True).then_inc(max_done, 1)
                        continue
                    if what == "inverse":
                        i, h = item
                        slot = (HEADS * i + h) % STAT_RING
                        dve.wait_ge(exp_done, r.score_no(i, h))
                        dve.reciprocal(row_inv[:, slot:slot + 1], row_sum[:, slot:slot + 1])\
                            .then_inc(inverse_done, 1)
                        continue
                    if what == "build":
                        layer, = item
                        dve.wait_ge(shared_done, r.shared_no(
                            ("unit", "v", 1) if layer < 2 else ("hidden", 0, 1, CHUNKS - 1)))
                        build_ffn_weights(layer)
                        continue
                    item, = item
                    name = item[0]
                    if name == "turn":
                        _, i, j = item
                        t = tri(i) + j
                        dve.wait_ge(turn_hi, TURNS * g + t + 1)
                        dve.tensor_tensor(pt_lo[:, t % PT_RING, :, :], ps_t[t % TURN_RING][:, :, :],
                                          pt_hi[:, t % PT_RING, :, :], ALU.subtract)\
                            .then_inc(turn_split, 1)
                    elif name == "weigh":
                        i = item[1]
                        dve.wait_ge(attn_hi, BLOCKS * g + i + 1)
                        dve.tensor_tensor(at_lo[:, i % ATTN_RING, :, :],
                                          ps_o[:, :].rearrange("p (h t) -> p h t", t=P),
                                          at_hi[:, i % ATTN_RING, :, :], ALU.subtract)\
                            .then_inc(attn_split, 1)
                    elif name == "unit":
                        _, piece, half = item
                        cols = slice(half * HALF, (half + 1) * HALF)
                        if piece == "v":
                            dve.wait_ge(shared_done, r.shared_no(item))
                            dve.tensor_copy(vt[:, cols], ps_m[:, :]).then_inc(shared_read, 1)
                            continue
                        dve.wait_ge(shared_hi, r.hi_no(item))
                        if piece == "k":
                            dve.tensor_tensor(k_lo[:, cols], ps_m[:, :], k_hi[:, cols],
                                              ALU.subtract).then_inc(shared_read, 1)
                        else:
                            h = int(piece[1])
                            dve.scalar_tensor_tensor(out=q_lo[:, h, cols], in0=ps_m[:, :],
                                                     scalar=SCALE, in1=q_hi[:, h, cols],
                                                     op0=ALU.mult, op1=ALU.subtract)\
                                .then_inc(shared_read, 1)
                    elif name == "vblocks":
                        half = item[1]
                        dve.wait_ge(shared_hi, r.hi_no(item))
                        dve.tensor_tensor(v_lo[:, half * 4:half * 4 + 4, :],
                                          ps_m[:, :].rearrange("p (b d) -> p b d", d=P),
                                          v_hi[:, half * 4:half * 4 + 4, :], ALU.subtract)\
                            .then_inc(shared_read, 1)
                    elif name == "dense":
                        i = item[1]
                        dve.wait_ge(shared_done, r.shared_no(item))
                        dve.wait_ge(shared_read, r.shared_no(item) - 1)
                        dve.tensor_tensor(y[:, i, :], ps_m[:, :], y[:, i, :], ALU.add)\
                            .then_inc(shared_read, 1)
                    elif name == "hidden":
                        _, layer, half, o = item
                        u = HIDDEN.index(item)
                        dve.wait_ge(shared_hi, r.hi_no(item))
                        if u >= H_RING:
                            dve.wait_ge(hidden_lo, u + 1 - H_RING)
                        dve.tensor_scalar(raw[:, H_SLOTS[u % H_RING], :], ps_m[:, :],
                                          scales_x2[:, layer:layer + 1], 0.0, ALU.mult, ALU.max)\
                            .then_inc(shared_read, 1)
                    elif name == "split":
                        piece = item[1]
                        slot = r.raw_slot(piece)
                        dve.wait_ge(w_hi_done, r.piece_no(piece))
                        if piece.startswith("wd"):
                            hi, lo = (w[:, int(piece[2]), :] for w in (wd_hi, wd_lo))
                        else:
                            hi, lo = (w[:, PIECES.index(piece), :, :].rearrange("p c d -> p (c d)")
                                      for w in (w_hi, w_lo))
                        dve.tensor_tensor(lo, raw[:, slot, :], hi, ALU.subtract).then_inc(w_split, 1)

            def build_ffn_weights(layer):
                slot = (K_PIECE + layer) % RAW
                bits = raw[:, slot, :].bitcast(U8).rearrange("p (c o) -> p c o", o=E)
                dve.wait_ge(raw_loaded[slot], 16 * ((K_PIECE + layer) // RAW + 1))
                same = CHUNKS if layer == 0 else CHUNKS - 1
                dve.tensor_scalar(ffn_w[layer][:, 0:same, :], bits[:, 0:same, :], 2.0, -1.0,
                                  ALU.mult, ALU.add).then_inc(ffn_w_built, 1)
                if layer:
                    dve.tensor_scalar(ffn_w[layer][:, same, :], bits[:, same, :], inh_mul[:, 0:1],
                                      inh_add[:, 0:1], ALU.mult, ALU.add).then_inc(ffn_w_built, 1)

            run("prologue", -1)
            with dve.Fori(0, GROUPS - 1) as g:
                run("body", g)
            run("last", GROUPS - 1)

            for b in range(BLOCKS):
                eb = e_buf[:, b % E_RING, :]
                dve.wait_ge(final_exp, b + 1)
                dve.scalar_tensor_tensor(out=y[:, b, :], in0=banks4[:, b % BANKS4, :],
                                         scalar=scales[:, 2:3], in1=y[:, b, :],
                                         op0=ALU.mult, op1=ALU.mult).then_inc(fin_step, 1)
                dve.tensor_scalar(eb, eb, 1.0, None, ALU.add).then_inc(fin_step, 1)
                dve.wait_ge(fin_step, 4 * b + 2)
                dve.reciprocal(eb, eb).then_inc(fin_step, 1)
                dve.wait_ge(fin_step, 4 * b + 3)
                dve.tensor_tensor(y[:, b, :], y[:, b, :], eb, ALU.mult).then_inc(fin_step, 1)

        @block.tensor
        def _(pe):
            def three(out, sta, mov, start, stop):
                (sta_hi, sta_lo), (mov_hi, mov_lo) = sta, mov
                pe.matmul(out, sta_hi, mov_hi, start=start, stop=False)
                pe.matmul(out, sta_hi, mov_lo, start=False, stop=False)
                return pe.matmul(out, sta_lo, mov_hi, start=False, stop=stop)

            pe.wait_ge(consts, 10)
            for b in range(BLOCKS):
                pe.wait_ge(xn_ready, b + 1)
                if b >= BANKS4:
                    pe.wait_ge(ln_lo, b + 1 - BANKS4)
                for c in range(CHUNKS):
                    mm = pe.transpose(banks4[:, b % BANKS4, c * P:(c + 1) * P],
                                      x_sb[:, b, c * P:(c + 1) * P], ident[:, :])
                mm.then_inc(ln_turned, 1)
            pe.wait_ge(ln_lo, BLOCKS)

            def run(kind, g):
                r = Run(kind, g, "pe")
                for item in r.items:
                    name = item[0]
                    if name == "scores":
                        _, i, h = item
                        if i in (0, 4):
                            pe.wait_ge(shared_read, r.shared0 + 1 + max(
                                r.order.index(("unit", p, i // 4)) for p in (f"q{h}", "k")))
                        if kind != "prologue":
                            pe.wait_ge(exp_done, r.score_no(i, h) - 1 - (HEADS * i + h)
                                       + score_exps(i, h))
                        rows = slice(i * P, (i + 1) * P)
                        width = (i + 1) * P
                        at0 = score_banks(i, h)[0] * E
                        for at in range(0, width, E):
                            cols = slice(at, min(at + E, width))
                            three(ps_s[:, at0 + cols.start:at0 + cols.stop],
                                  (q_hi[:, h, rows], q_lo[:, h, rows]), (k_hi[:, cols], k_lo[:, cols]),
                                  True, at + E < width)
                        pe.matmul(ps_s[:, at0 + rows.start:at0 + rows.stop], ident_b[:, :],
                                  mask_b[:, :], start=False, stop=True).then_inc(scores_done, 1)
                    elif name == "turn":
                        _, i, j = item
                        t = tri(i) + j
                        pe.wait_ge(turn_split, TURNS * g + t + 1)
                        if j == 0:
                            pe.wait_ge(normed, SCORES * g + HEADS * (i + 1))
                        for h in range(HEADS):
                            mm = pe.transpose(ps_t[t % TURN_RING][:, h, :],
                                              probs[i % 2][:, h, j * P:(j + 1) * P], ident[:, :])
                        mm.then_inc(turned, 1)
                    elif name == "weigh":
                        _, i, j = item
                        t = tri(i) + j
                        if (i, j) == (0, 0):
                            pe.wait_ge(shared_read, r.shared0)
                        if (i, j) == (4, 4):
                            pe.wait_ge(shared_read, r.shared_no(("vblocks", 1)))
                        if j == 0:
                            pe.wait_ge(attn_split, BLOCKS * g + i + 1)
                        pe.wait_ge(turn_split, TURNS * g + t + 1 + TURN_RING)
                        mm = three(ps_o[:, :], (v_hi[:, j, :], v_lo[:, j, :]),
                                   tuple(pt[:, t % PT_RING, :, :].rearrange("p h t -> p (h t)")
                                         for pt in (pt_hi, pt_lo)), j == 0, j == i)
                        if j == i:
                            mm.then_inc(weighed, 1)
                    elif name == "unit":
                        _, piece, half, c = item
                        no = r.shared_no(whole(item))
                        if c == 0:
                            if kind != "prologue" or no > 1:
                                pe.wait_ge(shared_read, no - 1)
                            if half == 0:
                                pe.wait_ge(w_split, r.piece_no(piece))
                        cols = slice(half * HALF, (half + 1) * HALF)
                        w = PIECES.index(piece)
                        mm = three(ps_m[:, :], (w_hi[:, w, c, :], w_lo[:, w, c, :]),
                                   (xn_hi[:, c, cols], xn_lo[:, c, cols]), c == 0, c == CHUNKS - 1)
                        if c == CHUNKS - 1:
                            mm.then_inc(shared_done, 1)
                    elif name == "vblocks":
                        half = item[1]
                        pe.wait_ge(shared_read, r.shared_no(item) - 1)
                        for n in range(4):
                            b = half * 4 + n
                            mm = pe.transpose(ps_m[:, n * P:(n + 1) * P], vt[:, b * P:(b + 1) * P],
                                              ident[:, :])
                        mm.then_inc(shared_done, 1)
                    elif name == "dense":
                        _, i, h = item
                        if h == 0:
                            pe.wait_ge(shared_read, r.shared_no(whole(item)) - 1)
                            pe.wait_ge(attn_split, BLOCKS * g + i + 2)
                            if i == 0:
                                pe.wait_ge(w_split, r.piece_no(f"wd{HEADS - 1}"))
                        mm = three(ps_m[:, :], (at_hi[:, i % ATTN_RING, h, :],
                                                at_lo[:, i % ATTN_RING, h, :]),
                                   (wd_hi[:, h, :], wd_lo[:, h, :]), h == 0, h == HEADS - 1)
                        if h == HEADS - 1:
                            mm.then_inc(shared_done, 1)
                    elif name == "hidden":
                        _, layer, half, o, c = item
                        if c == 0:
                            pe.wait_ge(shared_read, r.shared_no(whole(item)) - 1)
                            pe.wait_ge(ffn_w_built, 1 if layer == 0 else 3)
                            if layer:
                                pe.wait_ge(hidden_lo, HIDDEN.index(("hidden", 0, half, CHUNKS - 1)) + 1)
                        cols = slice(half * HALF, (half + 1) * HALF)
                        for part in (0, 1):
                            mm = pe.matmul(ps_m[:, :], ffn_w[layer][:, c, o * P:(o + 1) * P],
                                           ffn_in[layer][part][:, c, cols],
                                           start=(c == 0 and part == 0),
                                           stop=(c == CHUNKS - 1 and part == 1))
                        if c == CHUNKS - 1:
                            mm.then_inc(shared_done, 1)

            run("prologue", -1)
            with pe.Fori(0, GROUPS - 1) as g:
                run("body", g)
            run("last", GROUPS - 1)

            pe.wait_ge(ffn_w_built, 5)
            pe.wait_ge(exp_done, SCORES * GROUPS)
            pe.wait_ge(shared_read, PRO_SHARED + BODY_SHARED * (GROUPS - 1) + len(shared("last")))
            for b in range(BLOCKS):
                if b >= BANKS4:
                    pe.wait_ge(fin_step, 4 * (b - BANKS4) + 1)
                if b % 4 == 0:
                    pe.wait_ge(hidden_lo, HIDDEN.index(("hidden", 1, b // 4, CHUNKS - 1)) + 1)
                for c in range(CHUNKS):
                    for part in (0, 1):
                        mm = pe.matmul(banks4[:, b % BANKS4, :],
                                       ffn_in[2][part][:, c, b * P:(b + 1) * P], ffn_w[2][:, c, :],
                                       start=(c == 0 and part == 0), stop=(c == CHUNKS - 1 and part == 1))
                mm.then_inc(final_done, 1)


def kernel(**inputs):
    import numpy as np
    import concourse.bacc as bacc
    from concourse.bass_utils import run_bass_kernel_spmd

    x = np.ascontiguousarray(inputs["L0_attn_q"]).reshape(S, E)
    w = np.asarray(inputs["L0_attn_w_qkv"])
    wq = w[:GROUPS * HEADS * P].reshape(GROUPS, HEADS, P, CHUNKS, P)
    wk = w[GROUPS * HEADS * P:][:GROUPS * P].reshape(GROUPS, 1, P, CHUNKS, P)
    wv = w[(GROUPS * HEADS + GROUPS) * P:].reshape(GROUPS, 1, P, CHUNKS, P)
    wqkv = np.ascontiguousarray(np.concatenate([wq, wv, wk], 1).transpose(0, 1, 4, 3, 2))
    wqkv = wqkv.reshape(GROUPS, PRO_PIECES, P, E)
    wd = np.ascontiguousarray(np.asarray(inputs["L0_attn_w_dense"]).T).reshape(GROUPS, HEADS, P, E)
    arrays = {"x": x, "wqkv": wqkv, "wd": wd}
    for n in range(3):
        arrays[f"k{n}"] = np.ascontiguousarray(inputs[f"L0_ffn_k{n}"])
        arrays[f"s{n}"] = np.asarray(inputs[f"L0_ffn_s{n}"]).reshape(1)

    nc = bacc.Bacc("TRN2", target_bir_lowering=False, num_devices=1)
    ap = {name: nc.dram_tensor(name, a.shape, mybir.dt.from_np(a.dtype), kind="ExternalInput").ap()
          for name, a in arrays.items()}
    out = nc.dram_tensor("out", (S, E), F32, kind="ExternalOutput").ap()
    build(nc, ap["x"], ap["wqkv"], ap["wd"], [ap[f"k{n}"] for n in range(3)],
          [ap[f"s{n}"] for n in range(3)], out)
    result = run_bass_kernel_spmd(nc, [arrays], core_ids=[0]).results[0]["out"]
    return result.reshape(1, S, E)
```

```python
from contextlib import ExitStack

import concourse.bass as bass
from concourse import mybir

F32 = mybir.dt.float32
F32R = mybir.dt.float32r
BF16 = mybir.dt.bfloat16
U8 = mybir.dt.uint8
ACT = mybir.ActivationFunctionType
ALU = mybir.AluOpType

P = 128
S, E = 1024, 512
GROUPS, HEADS = 8, 4
BLOCKS = S // P
CHUNKS = E // P
HALF = S // 2
EPS = 1e-5
SCALE = float(P) ** -0.5
CONSTS = 9
WARM_UP = 36
MASKED = -1e37
BIG = 3e38
EXC = round(E * 0.8)
INH_FACTOR = -0.8 / (1.0 - 0.8)

RAW = 5
TURN_RING = 2
PT_RING = 4
ATTN_RING = 2
SILU_RING = 6
STAT_RING = 8

PIECES = ["q0", "q1", "q2", "q3", "v", "k"]
PRO_PIECES = len(PIECES)
BODY_PIECES = HEADS + PRO_PIECES


def tri(i):
    return i * (i + 1) // 2


TURNS = tri(BLOCKS)
SCORES = HEADS * BLOCKS


BUSY = 1e9
PASS, SHORT_PASS, SIGNAL = 0.216, 0.109, 0.21


def columns_cost(width):
    banks = len(score_banks(width // P - 1, 0))
    return 3 * banks * max(SHORT_PASS, PASS * width / banks / E)


def pe_queues(kind):
    last = kind == "last"
    unit = lambda piece, half: [("unit", piece, half, c) for c in range(CHUNKS)]
    nxt = sum((unit(p, 0) for p in PIECES), []) + [("vblocks", 0)]
    first_scores = [("scores", 0, h) for h in range(HEADS)]
    turns, weighs = ([(name, i, j) for i in range(BLOCKS) for j in range(i + 1)]
                     for name in ("turn", "weigh"))
    scores = [("scores", i, h) for i in range(1, BLOCKS) for h in range(HEADS)]
    units = sum((unit(p, 1) for p in ("q0", "k", "q1", "q2", "q3", "v")), []) + [("vblocks", 1)]
    dense = [("dense", i, h) for i in range(BLOCKS) for h in range(HEADS)]
    hidden = [("hidden", layer, half, o, c) for half in range(2) for layer in range(2)
              for o in range(CHUNKS) for c in range(CHUNKS)]
    if last:
        return [scores, turns, weighs, units, dense, hidden, [("final", b) for b in range(BLOCKS)]]
    return [scores + first_scores, turns, weighs, units + nxt, dense, []]


def pe_cost(item):
    kind = item[0]
    if kind == "scores":
        return columns_cost((item[1] + 1) * P)
    if kind in ("turn", "vblocks"):
        return 4 * SHORT_PASS
    return PASS * {"hidden": 2, "final": 2 * CHUNKS}.get(kind, 3)


def whole(item):
    return item[:-1] if item[0] in ("unit", "dense", "hidden") else item


def plan(kind, leads):
    queues = pe_queues(kind)
    total = [sum(map(pe_cost, q)) or 1 for q in queues]
    done, at = [0.0] * len(queues), [0] * len(queues)
    orders = {"pe": [], "act": [], "dve": [], "pool": []}
    free = {"act": 0.0, "dve": 0.0, "pool": 0.0}
    tasks = []
    there = {}
    end = {}
    bank = {"shared": 1.05}
    rows, ended = [], [0.0]
    t, number, open_item = 0.0, 0, None

    def task(at_time, engine, name, duration, then):
        nonlocal number
        number += 1
        tasks.append((at_time + SIGNAL, number, engine, name, duration, then))

    def chain(at_time, steps, then):
        engine, name, duration = steps[0]
        rest = steps[1:]
        task(at_time, engine, name, duration,
             (lambda e: chain(e, rest, then)) if rest else (lambda e: then(e + SIGNAL)))

    def advance(until):
        while tasks:
            best = min(tasks, key=lambda x: (max(free[x[2]], x[0]), x[0], x[1]))
            start = max(free[best[2]], best[0])
            if start > until:
                return
            tasks.remove(best)
            free[best[2]] = start + best[4]
            orders[best[2]].append(best[3])
            best[5](start + best[4])

    def row(b):
        if ("dense", b) in there and ("final", b) in there and b not in rows:
            rows.append(b)
            last_row = b == BLOCKS - 1
            chain(max(there[("dense", b)], there[("final", b)]) - SIGNAL, [("dve", ("gate", b), 0.6)],
                  lambda e: (there.update({("gated", b): e}), chain(
                      e - SIGNAL, [("dve", ("add_x", b), 0.6) if last_row else
                                   ("pool", ("add_x", b), 1.22)], ended.append)))

    def free_bank(*names):
        return lambda e: bank.update({n: e for n in names})

    def ready(item):
        what = item[0]
        if what == "scores":
            i, h = item[1:]
            half = i // 4
            if i == 0 and h and ("dense", BLOCKS - 2, HEADS - 1) not in end:
                return None
            if i in (0, 4):
                for p in ("k", f"q{h}"):
                    if ("unit", p, half) not in there:
                        return None
            if ("turn", (i - 2) % BLOCKS, (i - 2) % BLOCKS) not in end \
                    and i != 1:
                return None
            return max([bank.get(("score", b), 0.0) for b in score_banks(i, h)]
                       + [there[("unit", p, half)] for p in ("k", f"q{h}") if i in (0, 4)])
        if what == "turn":
            i, j = item[1:]
            if i and ("norm", i, HEADS - 1) not in there:
                return None
            n = tri(i) + j
            if n >= PT_RING and ("weigh", *pairs[n - PT_RING]) not in end:
                return None
            return max(bank.get(("turn", n % 2), 0.0), there.get(("norm", i, HEADS - 1), 0.0))
        if what == "weigh":
            i, j = item[1:]
            if item not in there or ((i, j) == (4, 4) and ("vblocks", 1) not in there):
                return None
            if i == j and i >= ATTN_RING and ("dense", i - ATTN_RING, HEADS - 1) not in end:
                return None
            return max(there[item], bank.get("attn", 0.0) if j == 0 else 0.0,
                       there[("vblocks", 1)] if (i, j) == (4, 4) else 0.0)
        if what == "final":
            b = item[1]
            needs = [("hidden", 1, b // 4, CHUNKS - 1), ("hidden", 0, 1, CHUNKS - 1), ("built", 2)]
            if ("scores", BLOCKS - 1, HEADS - 1) not in end \
                    or ("vblocks", 1) not in end \
                    or (b >= SILU_RING and ("gated", b - SILU_RING) not in there) \
                    or any(n not in there for n in needs):
                return None
            return max([bank.get(("score", b % 4), 0.0)] + [there[n] for n in needs])
        if open_item is not None:
            return 0.0 if open_item == whole(item) else None
        needs = []
        if what == "dense":
            if kind == "body" and item[1] == BLOCKS - 2 \
                    and ("weigh", BLOCKS - 1, BLOCKS - 1) not in end:
                return None
            needs = [("attn", item[1])] + ([("split", f"wd{HEADS - 1}")] if item[1] == 0 else [])
        elif what == "vblocks":
            needs = [("unit", "v", item[1])]
            if item[1] == 0 and ("weigh", BLOCKS - 1, 3) not in end:
                return None
        elif what == "unit" and item[2] == 0:
            needs = [("split", item[1])]
            if ("scores", 7 if item[1] == "k" else 3, HEADS - 1) not in end:
                return None
        elif what == "hidden":
            _, layer, half, o, c = item
            needs = [("built", layer)]
            if layer == 0 and ("scores", 4 * half + 3, HEADS - 1) not in end:
                return None
            if layer == 1:
                needs += [("hidden", 0, half, n) for n in range(CHUNKS)]
        if any(n not in there for n in needs):
            return None
        return max([bank.get("shared", 0.0)] + [there[n] for n in needs])

    pairs = [(i, j) for i in range(BLOCKS) for j in range(i + 1)]
    splits = [f"wd{n}" for n in range(HEADS)] + ([] if kind == "last" else PIECES)
    last_split = -9.0
    while any(at[q] < len(queue) for q, queue in enumerate(queues)):
        advance(t)
        if splits and t - last_split > 2.0:
            piece = splits[0]
            if piece.startswith("wd") \
                    or end.get(("unit", piece, 1, CHUNKS - 1), 1e9) < t:
                splits.pop(0)
                last_split = t
                chain(t, [("act", ("hi", ("split", piece)), 0.62), ("dve", ("lo", ("split", piece)), 0.6)],
                      lambda e, p=piece: there.update({("split", p): e}))
        choice = [(q, ready(queue[at[q]])) for q, queue in enumerate(queues) if at[q] < len(queue)]
        now = [(done[q] / total[q] - leads[q], q) for q, r in choice if r is not None and r <= t]
        if not now:
            t += 0.04
            continue
        _, q = min(now)
        item = queues[q][at[q]]
        at[q] += 1
        done[q] += pe_cost(item)
        t += pe_cost(item) + 0.003
        end[item] = t
        orders["pe"].append(item)
        what = item[0]
        if what == "scores":
            i, h = item[1:]
            w = (i + 1) * P
            bank.update({("score", b): BUSY for b in score_banks(i, h)})

            def after_exp(e, i=i, h=h, w=w):
                free_bank(*[("score", b) for b in score_banks(i, h)])(e + SIGNAL)
                chain(e, [("dve", ("inverse", i, h), 0.07), ("pool", ("norm", i, h), 0.15 + w / 440)],
                      lambda e2: there.update({("norm", i, h): e2}))
            task(t, "dve", ("max", i, h), 0.125 + w / 960,
                 lambda e, i=i, h=h, w=w, f=after_exp: task(e, "act", ("exp", i, h), 0.25 + w / 1200, f))
        elif what == "turn":
            i, j = item[1:]
            bank[("turn", (tri(i) + j) % 2)] = BUSY

            def turn_split_at(e, i=i, j=j):
                bank[("turn", (tri(i) + j) % 2)] = e
                there[("weigh", i, j)] = e
            chain(t, [("act", ("hi", item), 0.48), ("dve", ("lo", item), 0.61)], turn_split_at)
        elif what == "weigh" and item[1] == item[2]:
            bank["attn"] = BUSY
            chain(t, [("act", ("hi", item), 0.48), ("dve", ("lo", item), 0.61)],
                  lambda e, i=item[1]: (bank.update({"attn": e}), there.update({("attn", i): e})))
        elif what == "final":
            b = item[1]
            bank[("score", b % 4)] = BUSY
            chain(t, [("act", ("silu", b), 0.48)],
                  lambda e, b=b: (bank.update({("score", b % 4): e}), there.update({("final", b): e}),
                                  row(b)))
        elif what in ("unit", "dense", "hidden", "vblocks"):
            open_item = whole(item) if what != "vblocks" and item[-1] < CHUNKS - 1 else None
            if open_item is None:
                w = whole(item)
                steps = [("act", ("hi", w), 0.48)] if has_hi(w) else []
                steps += [("dve", ("lo", w), 0.61)]
                bank["shared"] = BUSY
                if what == "hidden":
                    chain(t, steps, lambda e, w=w: (bank.update({"shared": e}), chain(
                        e, [("pool", ("low", w), 1.25)], lambda e2, w=w: there.update({w: e2}))))
                else:
                    chain(t, steps, lambda e, w=w: (bank.update({"shared": e}), there.update({w: e}),
                                                    row(w[1]) if kind == "last" else None))
                if kind == "last" and w == ("unit", "v", 1):
                    for layer in range(3):
                        chain(t, [("dve", ("build", layer), 2.2)],
                              lambda e, n=layer: there.update({("built", n): e}))
    for piece in splits:
        chain(t, [("act", ("hi", ("split", piece)), 0.62), ("dve", ("lo", ("split", piece)), 0.6)],
              lambda e: None)
    advance(1e9)
    return max([t] + ended), orders


def score_banks(i, h):
    return [h] if (i + 1) * P <= E else [2 * (h % 2), 2 * (h % 2) + 1]


def has_hi(item):
    return item[0] in ("vblocks", "hidden") or (item[0] == "unit" and item[1] != "v")


def score_exps(i, h):
    n = HEADS * i + h
    back = 1
    while not set(score_banks(i, h)) & set(score_banks((n - back) // HEADS % BLOCKS,
                                                       (n - back) % HEADS)):
        back += 1
    return n - back + 1


def prologue():
    unit = lambda piece: [("unit", piece, 0, c) for c in range(CHUNKS)]
    ln = lambda *blocks: [("ln", b) for b in blocks]
    values = [("vblocks", 0)]
    pe = ln(0, 1, 2, 3) + unit("q0") + unit("q1") + ln(4, 5) + unit("q2") + ln(6, 7) \
        + unit("q3") + unit("k") + unit("v") + [("scores", 0, h) for h in range(HEADS)] + values
    units = [("unit", p, 0) for p in ("q0", "q1", "q2", "q3", "k", "v")]
    hi = lambda *items: [("hi", item) for item in items]
    lo = lambda *items: [("lo", item) for item in items]
    split = [("split", p) for p in PIECES]
    act = [("root", 0)] + hi(split[0], split[1], *ln(0, 1, 2, 3), *split[2:], units[0]) \
        + [("root", 1)] + hi(units[1], *ln(4, 5), units[2], *ln(6, 7), *units[3:5]) \
        + [("exp", 0, h) for h in range(HEADS)] + hi(*values)
    stats, scaled = ([(name, b) for b in range(BLOCKS)] for name in ("stats", "scale"))
    dve = stats[:4] + [("moments", 0)] + scaled[:4] + lo(*ln(0, 1, 2, 3)) \
        + stats[4:] + [("moments", 1)] + lo(units[0]) + scaled[4:] \
        + lo(units[1], *ln(4, 5), units[2], *ln(6, 7), *units[3:]) + [("ffn_scales",)]
    for name in ("max", "inverse"):
        dve += [(name, 0, h) for h in range(HEADS)]
    dve += lo(*values)
    pool = lo(*split) + [("zero_y",)] + [("norm", 0, h) for h in range(HEADS)]
    return {"pe": pe, "act": act, "dve": dve, "pool": pool}


ORDERS = {"prologue": prologue(),
          "body": plan("body", (-0.12, -0.22, -0.38, 0.04, -0.44, 0))[1],
          "last": plan("last", (-1.29, -0.41, -1.57, 0.54, 0.76, -0.26, -0.81))[1]}
ROWS = [i[1] for i in ORDERS["last"]["dve"] if i[0] == "gate"]


def shared(kind):
    return [whole(i) for i in ORDERS[kind]["pe"]
            if i[0] == "vblocks" or (i[0] in ("unit", "dense", "hidden") and i[-1] == CHUNKS - 1)]


PRO_SHARED, BODY_SHARED = len(shared("prologue")), len(shared("body"))
PRO_HI = sum(map(has_hi, shared("prologue")))
BODY_HI = sum(map(has_hi, shared("body")))


class Run:

    def __init__(self, kind, g, engine):
        pro = kind == "prologue"
        self.kind, self.g, self.items = kind, g, ORDERS[kind][engine]
        self.shared0 = 0 if pro else PRO_SHARED + BODY_SHARED * g
        self.hi0 = 0 if pro else PRO_HI + BODY_HI * g
        self.piece0 = 0 if pro else PRO_PIECES + BODY_PIECES * g
        self.order = shared(kind)
        self.his = [i for i in self.order if has_hi(i)]
        self.splits = [i[1][1] for i in ORDERS[kind]["act"] if i[0] == "hi" and i[1][0] == "split"]

    def bank_free(self, no):
        return no - 2 if self.kind == "prologue" else no - 1

    def shared_no(self, item):
        return self.shared0 + self.order.index(item) + 1

    def hi_no(self, item):
        return self.hi0 + self.his.index(item) + 1

    def piece_no(self, piece):
        return self.piece0 + self.splits.index(piece) + 1

    def score_no(self, i, h):
        return SCORES * (self.g + 1 if i == 0 else self.g) + HEADS * i + h + 1

    def raw_slot(self, piece):
        n = self.splits.index(piece)
        return (n if self.kind == "prologue" else PRO_PIECES + n) % RAW

    def raw_turn(self, piece):
        n = self.splits.index(piece)
        return n // RAW + 1 if self.kind == "prologue" else \
            (PRO_PIECES + n) // RAW + 1 + BODY_PIECES // RAW * self.g


LOAD_X_BEFORE = {0: (0, 1, 2, 3), 2: (4, 5), 3: (6, 7)}
K_PIECE = PRO_PIECES + BODY_PIECES * (GROUPS - 1) + HEADS
HIDDEN = [w for w in shared("last") if w[0] == "hidden"]


def build(nc, x_d, wqkv_d, wd_d, k_ds, s_ds, out_d):
    assert BODY_PIECES % RAW == 0
    assert TURNS % TURN_RING == 0 and TURNS % PT_RING == 0
    ctx = ExitStack()
    with ctx:
        def sb(name, shape, dt=F32):
            return ctx.enter_context(nc.sbuf_tensor(name, shape, dt))

        def ps(name, shape):
            return ctx.enter_context(nc.psum_tensor(name, shape, F32))

        def sem(name):
            return ctx.enter_context(nc.semaphore(name))

        xn_hi = sb("xn_hi", [P, CHUNKS, S], F32R)
        xn_lo = sb("xn_lo", [P, CHUNKS, S], F32R)
        y = sb("y", [P, BLOCKS, E])
        raw = sb("raw", [P, RAW, E])
        w_hi = sb("w_hi", [P, PRO_PIECES, CHUNKS, P], F32R)
        w_lo = sb("w_lo", [P, PRO_PIECES, CHUNKS, P], F32R)
        wd_hi = sb("wd_hi", [P, HEADS, E], F32R)
        wd_lo = sb("wd_lo", [P, HEADS, E], F32R)
        q_hi = sb("q_hi", [P, HEADS, S], F32R)
        q_lo = sb("q_lo", [P, HEADS, S], F32R)
        k_hi = sb("k_hi", [P, S], F32R)
        k_lo = sb("k_lo", [P, S], F32R)
        vt = sb("vt", [P, S])
        v_hi = sb("v_hi", [P, BLOCKS, P], F32R)
        v_lo = sb("v_lo", [P, BLOCKS, P], F32R)
        prob_even = sb("prob_even", [P, HEADS, S - P])
        prob_odd = sb("prob_odd", [P, HEADS, S])
        pt_hi = sb("pt_hi", [P, PT_RING, HEADS, P], F32R)
        pt_lo = sb("pt_lo", [P, PT_RING, HEADS, P], F32R)
        at_hi = sb("at_hi", [P, ATTN_RING, HEADS, P], F32R)
        at_lo = sb("at_lo", [P, ATTN_RING, HEADS, P], F32R)
        ident = sb("ident", [P, P])
        mask = sb("mask", [P, S], BF16)
        neg_max = sb("neg_max", [P, STAT_RING])
        row_sum = sb("row_sum", [P, STAT_RING])
        row_inv = sb("row_inv", [P, STAT_RING])
        bn = sb("bn", [P, BLOCKS, 6])
        mv = sb("mv", [P, BLOCKS, 2])
        var_eps = sb("var_eps", [P, BLOCKS])
        std = sb("std", [P, BLOCKS])
        rstd = sb("rstd", [P, BLOCKS])
        half_var = sb("half_var", [P, BLOCKS])
        newton = sb("newton", [P, BLOCKS])
        scales = sb("scales", [P, 3])
        scales_x2 = sb("scales_x2", [P, 3])
        credit = sb("credit", [P, 2])
        inh_mul = sb("inh_mul", [P, 1])
        inh_add = sb("inh_add", [P, 1])

        probs = (prob_even, prob_odd)
        x_sb = prob_odd[:, :, :].rearrange("p h (a e) -> p (h a) e", e=E)
        x_even = prob_even[:, :, :].rearrange("p h s -> p (h s)").rearrange("p (b e) -> p b e", e=E)
        x_back = [x_even[:, b, :] for b in range(BLOCKS - 1)] + [raw[:, K_PIECE % RAW, :]]
        H_SLOTS = [(K_PIECE - n) % RAW for n in (2, 1)]
        H_RING = len(H_SLOTS)
        w_rows = [w[:, :, :, :].rearrange("p n c d -> p n (c d)") for w in (w_hi, w_lo)]
        ffn_w = [[w_rows[0][:, c, :] for c in range(CHUNKS)], [w_rows[1][:, c, :] for c in range(CHUNKS)],
                 [w_rows[c // 2][:, CHUNKS + c % 2, :] for c in range(CHUNKS)]]
        silu = [vt[:, 0:E], vt[:, E:2 * E]] \
            + [raw[:, slot, :] for slot in ((K_PIECE + 1) % RAW, (K_PIECE + 2) % RAW, *H_SLOTS)]
        ffn_in = ((xn_hi, xn_lo), (q_hi, q_lo), (xn_hi, xn_lo))

        BANKS4 = 4
        ps_s = ps("ps_s", [P, BANKS4 * E])
        ps_t = [ps(f"ps_t{n}", [P, HEADS, P]) for n in range(TURN_RING)]
        ps_o = ps("ps_o", [P, HEADS * P])
        ps_m = ps("ps_m", [P, E])
        banks4 = ps_s[:, :].rearrange("p (n e) -> p n e", e=E)

        def score_rows(i, h):
            banks = score_banks(i, h)
            width = (i + 1) * P // len(banks)
            cut = lambda ap: ap.rearrange("p (n e) -> p n e", e=width)
            return banks4[:, banks[0]:banks[0] + len(banks), 0:width], cut

        def shared_bank(run, item):
            if run.kind == "prologue" and item in run.order and run.order.index(item) % 2:
                return ps_o
            return ps_m

        x_loaded = [sem(f"x_loaded{b}") for b in range(BLOCKS)]
        scales_loaded = sem("scales_loaded")
        raw_loaded = [sem(f"raw_loaded{n}") for n in range(RAW)]
        stored = sem("stored")
        consts = sem("consts")
        ln_stats = sem("ln_stats")
        ln_moments = sem("ln_moments")
        ln_step = sem("ln_step")
        ln_sqrt = sem("ln_sqrt")
        ln_turned = sem("ln_turned")
        ln_hi = sem("ln_hi")
        ln_lo = sem("ln_lo")
        xn_ready = sem("xn_ready")
        w_hi_done = sem("w_hi_done")
        w_split = sem("w_split")
        shared_done = sem("shared_done")
        shared_hi = sem("shared_hi")
        shared_read = sem("shared_read")
        scores_done = sem("scores_done")
        scores_seen = sem("scores_seen")
        max_done = sem("max_done")
        exp_done = sem("exp_done")
        inverse_done = sem("inverse_done")
        normed = sem("normed")
        turned = sem("turned")
        turn_hi = sem("turn_hi")
        turn_split = sem("turn_split")
        weighed = sem("weighed")
        attn_hi = sem("attn_hi")
        attn_split = sem("attn_split")
        ffn_w_built = sem("ffn_w_built")
        hidden_lo = sem("hidden_lo")
        final_done = sem("final_done")
        silu_done = sem("silu_done")
        gated = sem("gated")
        scaled = sem("scaled")
        row_ready = sem("row_ready")
        last_row_ready = sem("last_row_ready")

        LN_STEPS = 6

        block = ctx.enter_context(nc.Block())

        @block.sync
        def _(sp):
            def load_x(*blocks):
                for b in blocks:
                    sp.dma_start(x_sb[:, b, :], x_d[b * P:(b + 1) * P, :]).then_inc(x_loaded[b], 16)

            def load(kind, g):
                run = Run(kind, g, "act")
                for n, piece in enumerate(run.splits):
                    if kind == "prologue" and n in LOAD_X_BEFORE:
                        load_x(*LOAD_X_BEFORE[n])
                    if kind != "prologue" or n >= RAW:
                        sp.wait_ge(w_split, run.piece0 + n + 1 - RAW)
                    if piece.startswith("wd"):
                        src = wd_d[bass.ds(g, 1), int(piece[2]), :, :]
                    else:
                        src = wqkv_d[bass.ds(g + 1, 1), PIECES.index(piece), :, :]
                    slot = run.raw_slot(piece)
                    sp.dma_start(raw[:, slot, :], src.rearrange("a p e -> (a p) e"))\
                      .then_inc(raw_loaded[slot], 16)

            load("prologue", -1)
            for n, s_d in enumerate(s_ds):
                sp.dma_start(scales[:, n:n + 1], s_d.partition_broadcast(P)).then_inc(scales_loaded, 16)
            with sp.Fori(0, GROUPS - 1) as g:
                load("body", g)
            load("last", GROUPS - 1)
            for n, k_d in enumerate(k_ds):
                sp.wait_ge(w_split, K_PIECE + n + 1 - RAW)
                slot = (K_PIECE + n) % RAW
                sp.dma_start(raw[:, slot, :].bitcast(U8).rearrange("p (c o) -> p c o", o=E),
                             k_d.rearrange("(c p) o -> p c o", p=P)).then_inc(raw_loaded[slot], 16)
            for b in (BLOCKS - 1, *range(BLOCKS - 1)):
                if b == BLOCKS - 1:
                    sp.wait_ge(ffn_w_built, CHUNKS)
                if b == 0:
                    sp.wait_ge(turned, TURNS * GROUPS - BLOCKS)
                sp.dma_start(x_back[b], x_d[b * P:(b + 1) * P, :]).then_inc(x_loaded[b], 16)
            for n, b in enumerate(ROWS):
                if b == BLOCKS - 1:
                    sp.wait_ge(last_row_ready, 1)
                else:
                    sp.wait_ge(row_ready, n + 1)
                sp.dma_start(out_d[b * P:(b + 1) * P, :], y[:, b, :]).then_inc(stored, 16)
            sp.wait_ge(stored, 16 * BLOCKS)

        @block.gpsimd
        def _(pool):
            pool.memset(ident[:, :], 0.0).then_inc(consts, 1)
            pool.memset(mask[:, :], 0.0).then_inc(consts, 1)
            pool.memset(inh_mul[:, :], 2.0).then_inc(consts, 1)
            pool.memset(inh_add[:, :], -1.0).then_inc(consts, 1)
            pool.wait_ge(consts, 4)
            pool.affine_select(out=ident[:, :], in_=ident[:, :], compare_op=ALU.not_equal, fill=1.0,
                               base=0, pattern=[[-1, P]], channel_multiplier=1).then_inc(consts, 1)
            diagonal = mask[:, S - P:S]
            pool.affine_select(out=diagonal, in_=diagonal, compare_op=ALU.is_ge, fill=MASKED,
                               base=0, pattern=[[-1, P]], channel_multiplier=1).then_inc(consts, 1)
            first = EXC - (CHUNKS - 1) * P
            for m, v in ((inh_mul, 2.0 * INH_FACTOR), (inh_add, -INH_FACTOR)):
                pool.affine_select(out=m[:, :], in_=m[:, :], compare_op=ALU.is_ge, fill=v,
                                   base=first - 1, pattern=[[0, 1]], channel_multiplier=-1)\
                    .then_inc(consts, 1)

            def run(kind, g):
                r = Run(kind, g, "pool")
                for what, *item in r.items:
                    if what == "norm":
                        i, h = item
                        slot = (HEADS * i + h) % STAT_RING
                        rows = probs[i % 2][:, h, 0:(i + 1) * P]
                        pool.wait_ge(inverse_done, r.score_no(i, h))
                        pool.tensor_tensor(rows, rows, row_inv[:, slot:slot + 1]
                                           .to_broadcast([P, (i + 1) * P]), ALU.mult)\
                            .then_inc(normed, 1)
                    elif what == "lo":
                        piece = item[0][1]
                        pool.wait_ge(w_hi_done, r.piece_no(piece))
                        hi, lo = (w[:, PIECES.index(piece), :, :].rearrange("p c d -> p (c d)")
                                  for w in (w_hi, w_lo))
                        pool.tensor_tensor(lo, raw[:, r.raw_slot(piece), :], hi, ALU.subtract)\
                            .then_inc(w_split, 1)
                    elif what == "zero_y":
                        pool.memset(y[:, :, :], 0.0).then_inc(consts, 1)
                    elif what == "add_x":
                        b, = item
                        pool.wait_ge(x_loaded[b], 16 * 2)
                        pool.wait_ge(gated, ROWS.index(b) + 1)
                        pool.tensor_tensor(y[:, b, :], y[:, b, :], x_back[b], ALU.add)\
                            .then_inc(row_ready, 1)
                    elif what == "low":
                        _, layer, half, o = item[0]
                        hi, lo = ffn_in[layer + 1]
                        cols = slice(half * HALF, (half + 1) * HALF)
                        u = HIDDEN.index(item[0])
                        pool.wait_ge(shared_read, r.shared_no(item[0]))
                        pool.tensor_tensor(lo[:, o, cols], raw[:, H_SLOTS[u % H_RING], :],
                                           hi[:, o, cols], ALU.subtract).then_inc(hidden_lo, 1)

            run("prologue", -1)
            with pool.Fori(0, GROUPS - 1) as g:
                run("body", g)
            run("last", GROUPS - 1)

        @block.scalar
        def _(act):
            def run(kind, g):
                r = Run(kind, g, "act")
                for what, *item in r.items:
                    if what == "exp":
                        i, h = item
                        slot = (HEADS * i + h) % STAT_RING
                        scores, halves = score_rows(i, h)
                        act.wait_ge(max_done, r.score_no(i, h))
                        act.activation(halves(probs[i % 2][:, h, 0:(i + 1) * P]), scores,
                                       ACT.Exp, scale=-1.0, bias=neg_max[:, slot:slot + 1],
                                       accum_out=row_sum[:, slot:slot + 1]).then_inc(exp_done, 1)
                        continue
                    if what == "silu":
                        b, = item
                        act.wait_ge(final_done, b + 1)
                        if b >= SILU_RING:
                            act.wait_ge(gated, ROWS.index(b - SILU_RING) + 1)
                        act.activation(silu[b % SILU_RING], banks4[:, b % BANKS4, :], ACT.Silu,
                                       scale=scales[:, 2:3]).then_inc(silu_done, 1)
                        continue
                    if what == "root":
                        half = slice(item[0] * 4, item[0] * 4 + 4)
                        act.wait_ge(ln_step, LN_STEPS * item[0] + 1)
                        act.activation(std[:, half], var_eps[:, half], ACT.Sqrt).then_inc(ln_sqrt, 1)
                        continue
                    item, = item
                    name = item[0]
                    bank = shared_bank(r, item)
                    if name == "ln":
                        b = item[1]
                        act.wait_ge(ln_turned, b + 1)
                        act.activation(xn_hi[:, :, b * P:(b + 1) * P],
                                       banks4[:, b % BANKS4, :].rearrange("p (c t) -> p c t", t=P),
                                       ACT.Copy).then_inc(ln_hi, 1)
                    elif name == "turn":
                        _, i, j = item
                        t = tri(i) + j
                        act.wait_ge(turned, TURNS * g + t + 1)
                        act.activation(pt_hi[:, t % PT_RING, :, :], ps_t[t % TURN_RING][:, :, :],
                                       ACT.Copy).then_inc(turn_hi, 1)
                    elif name == "weigh":
                        i = item[1]
                        act.wait_ge(weighed, BLOCKS * g + i + 1)
                        act.activation(at_hi[:, i % ATTN_RING, :, :],
                                       ps_o[:, :].rearrange("p (h t) -> p h t", t=P),
                                       ACT.Copy).then_inc(attn_hi, 1)
                    elif name == "unit":
                        _, piece, half = item
                        cols = slice(half * HALF, (half + 1) * HALF)
                        act.wait_ge(shared_done, r.shared_no(item))
                        if piece == "k":
                            act.activation(k_hi[:, cols], bank[:, :], ACT.Copy).then_inc(shared_hi, 1)
                        else:
                            act.activation(q_hi[:, int(piece[1]), cols], bank[:, :], ACT.Copy,
                                           scale=SCALE).then_inc(shared_hi, 1)
                    elif name == "vblocks":
                        half = item[1]
                        act.wait_ge(shared_done, r.shared_no(item))
                        act.activation(v_hi[:, half * 4:half * 4 + 4, :],
                                       bank[:, :].rearrange("p (b d) -> p b d", d=P),
                                       ACT.Copy).then_inc(shared_hi, 1)
                    elif name == "hidden":
                        _, layer, half, o = item
                        act.wait_ge(shared_done, r.shared_no(item))
                        act.activation(ffn_in[layer + 1][0][:, o, half * HALF:(half + 1) * HALF],
                                       bank[:, :], ACT.Relu, scale=scales_x2[:, layer:layer + 1])\
                            .then_inc(shared_hi, 1)
                    elif name == "split":
                        piece = item[1]
                        slot = r.raw_slot(piece)
                        act.wait_ge(raw_loaded[slot], 16 * r.raw_turn(piece))
                        if piece.startswith("wd"):
                            act.wait_ge(shared_done, r.shared0)
                            dst = wd_hi[:, int(piece[2]), :]
                        else:
                            if kind != "prologue":
                                act.wait_ge(shared_done, r.shared_no(("unit", piece, 1)))
                            dst = w_hi[:, PIECES.index(piece), :, :].rearrange("p c d -> p (c d)")
                        act.activation(dst, raw[:, slot, :], ACT.Copy).then_inc(w_hi_done, 1)

            run("prologue", -1)
            with act.Fori(0, GROUPS - 1) as g:
                run("body", g)
            act.wait_ge(scaled, 1)
            run("last", GROUPS - 1)

        @block.vector
        def _(dve):
            dve.memset(credit[:, 0:1], 0.0).then_inc(turn_split, TURN_RING)
            dve.memset(credit[:, 1:2], 0.0).then_inc(attn_split, 1)

            def moments(half):
                blocks = slice(half * 4, half * 4 + 4)
                base = LN_STEPS * half
                for b in range(BLOCKS)[blocks]:
                    dve.wait_ge(ln_stats, b + 1)
                    dve.bn_aggr(mv[:, b, :], bn[:, b, :]).then_inc(ln_moments, 1)
                dve.wait_ge(ln_moments, 4 * half + 4)
                dve.tensor_scalar(var_eps[:, blocks], mv[:, blocks, 1], EPS, None, ALU.add)\
                    .then_inc(ln_step, 1)
                dve.wait_ge(ln_step, base + 1)
                dve.tensor_scalar(half_var[:, blocks], var_eps[:, blocks], -0.5, None, ALU.mult)\
                    .then_inc(ln_step, 1)
                dve.wait_ge(ln_sqrt, half + 1)
                dve.reciprocal(rstd[:, blocks], std[:, blocks]).then_inc(ln_step, 1)
                dve.wait_ge(ln_step, base + 3)
                dve.tensor_tensor(newton[:, blocks], rstd[:, blocks], rstd[:, blocks], ALU.mult)\
                    .then_inc(ln_step, 1)
                dve.wait_ge(ln_step, base + 4)
                dve.tensor_tensor(newton[:, blocks], newton[:, blocks], half_var[:, blocks], ALU.mult)\
                    .then_inc(ln_step, 1)
                dve.wait_ge(ln_step, base + 5)
                dve.scalar_tensor_tensor(out=rstd[:, blocks], in0=newton[:, blocks], scalar=1.5,
                                         in1=rstd[:, blocks], op0=ALU.add, op1=ALU.mult)\
                    .then_inc(ln_step, 1)

            def run(kind, g):
                r = Run(kind, g, "dve")
                for what, *item in r.items:
                    if what == "max":
                        i, h = item
                        slot = (HEADS * i + h) % STAT_RING
                        scores, halves = score_rows(i, h)
                        dve.wait_ge(scores_done, r.score_no(i, h))
                        dve.sem_inc(scores_seen)
                        dve.tensor_tensor_reduce(
                            out=scores, in0=scores, in1=halves(mask[:, S - (i + 1) * P:S]),
                            scale=-1.0, scalar=BIG, op0=ALU.add, op1=ALU.min,
                            accum_out=neg_max[:, slot:slot + 1]).then_inc(max_done, 1)
                        continue
                    if what == "inverse":
                        i, h = item
                        slot = (HEADS * i + h) % STAT_RING
                        dve.wait_ge(exp_done, r.score_no(i, h))
                        dve.reciprocal(row_inv[:, slot:slot + 1], row_sum[:, slot:slot + 1])\
                            .then_inc(inverse_done, 1)
                        continue
                    if what == "stats":
                        b, = item
                        dve.wait_ge(x_loaded[b], 16)
                        dve.bn_stats(bn[:, b, :], x_sb[:, b, :]).then_inc(ln_stats, 1)
                        continue
                    if what == "moments":
                        moments(item[0])
                        continue
                    if what == "scale":
                        b, = item
                        dve.wait_ge(ln_step, LN_STEPS * (b // 4 + 1))
                        dve.tensor_scalar(x_sb[:, b, :], x_sb[:, b, :], mv[:, b, 0:1],
                                          rstd[:, b:b + 1], ALU.subtract, ALU.mult)\
                            .then_inc(xn_ready, 1)
                        continue
                    if what == "ffn_scales":
                        dve.wait_ge(scales_loaded, 16 * 3)
                        dve.tensor_scalar(scales_x2[:, :], scales[:, :], 2.0, None, ALU.mult)\
                            .then_inc(scaled, 1)
                        dve.wait_ge(consts, CONSTS - 1)
                        continue
                    if what == "gate":
                        b, = item
                        dve.wait_ge(silu_done, b + 1)
                        dve.wait_ge(shared_read, r.shared_no(("dense", b)))
                        dve.tensor_tensor(y[:, b, :], y[:, b, :], silu[b % SILU_RING], ALU.mult)\
                            .then_inc(gated, 1)
                        continue
                    if what == "add_x":
                        b, = item
                        dve.wait_ge(x_loaded[b], 16 * 2)
                        dve.wait_ge(gated, ROWS.index(b) + 1)
                        dve.tensor_tensor(y[:, b, :], y[:, b, :], x_back[b], ALU.add)\
                            .then_inc(last_row_ready, 1)
                        continue
                    if what == "build":
                        layer, = item
                        dve.wait_ge(shared_done, r.shared_no(("unit", "v", 1)))
                        build_ffn_weights(layer)
                        continue
                    item, = item
                    name = item[0]
                    bank = shared_bank(r, item)
                    if name == "ln":
                        b = item[1]
                        dve.wait_ge(ln_hi, b + 1)
                        dve.tensor_tensor(xn_lo[:, :, b * P:(b + 1) * P],
                                          banks4[:, b % BANKS4, :].rearrange("p (c t) -> p c t", t=P),
                                          xn_hi[:, :, b * P:(b + 1) * P], ALU.subtract)\
                            .then_inc(ln_lo, 1)
                    elif name == "turn":
                        _, i, j = item
                        t = tri(i) + j
                        dve.wait_ge(turn_hi, TURNS * g + t + 1)
                        dve.tensor_tensor(pt_lo[:, t % PT_RING, :, :], ps_t[t % TURN_RING][:, :, :],
                                          pt_hi[:, t % PT_RING, :, :], ALU.subtract)\
                            .then_inc(turn_split, 1)
                    elif name == "weigh":
                        i = item[1]
                        dve.wait_ge(attn_hi, BLOCKS * g + i + 1)
                        dve.tensor_tensor(at_lo[:, i % ATTN_RING, :, :],
                                          ps_o[:, :].rearrange("p (h t) -> p h t", t=P),
                                          at_hi[:, i % ATTN_RING, :, :], ALU.subtract)\
                            .then_inc(attn_split, 1)
                    elif name == "unit":
                        _, piece, half = item
                        cols = slice(half * HALF, (half + 1) * HALF)
                        if piece == "v":
                            dve.wait_ge(shared_done, r.shared_no(item))
                            dve.tensor_copy(vt[:, cols], bank[:, :]).then_inc(shared_read, 1)
                            continue
                        dve.wait_ge(shared_hi, r.hi_no(item))
                        if piece == "k":
                            dve.tensor_tensor(k_lo[:, cols], bank[:, :], k_hi[:, cols],
                                              ALU.subtract).then_inc(shared_read, 1)
                        else:
                            h = int(piece[1])
                            dve.scalar_tensor_tensor(out=q_lo[:, h, cols], in0=bank[:, :],
                                                     scalar=SCALE, in1=q_hi[:, h, cols],
                                                     op0=ALU.mult, op1=ALU.subtract)\
                                .then_inc(shared_read, 1)
                    elif name == "vblocks":
                        half = item[1]
                        dve.wait_ge(shared_hi, r.hi_no(item))
                        dve.tensor_tensor(v_lo[:, half * 4:half * 4 + 4, :],
                                          bank[:, :].rearrange("p (b d) -> p b d", d=P),
                                          v_hi[:, half * 4:half * 4 + 4, :], ALU.subtract)\
                            .then_inc(shared_read, 1)
                    elif name == "dense":
                        i = item[1]
                        dve.wait_ge(shared_done, r.shared_no(item))
                        dve.wait_ge(shared_read, r.shared_no(item) - 1)
                        dve.tensor_tensor(y[:, i, :], bank[:, :], y[:, i, :], ALU.add)\
                            .then_inc(shared_read, 1)
                    elif name == "hidden":
                        _, layer, half, o = item
                        u = HIDDEN.index(item)
                        dve.wait_ge(shared_hi, r.hi_no(item))
                        if u >= H_RING:
                            dve.wait_ge(hidden_lo, u + 1 - H_RING)
                        dve.tensor_scalar(raw[:, H_SLOTS[u % H_RING], :], bank[:, :],
                                          scales_x2[:, layer:layer + 1], 0.0, ALU.mult, ALU.max)\
                            .then_inc(shared_read, 1)
                    elif name == "split":
                        piece = item[1]
                        slot = r.raw_slot(piece)
                        dve.wait_ge(w_hi_done, r.piece_no(piece))
                        if piece.startswith("wd"):
                            hi, lo = (w[:, int(piece[2]), :] for w in (wd_hi, wd_lo))
                        else:
                            hi, lo = (w[:, PIECES.index(piece), :, :].rearrange("p c d -> p (c d)")
                                      for w in (w_hi, w_lo))
                        dve.tensor_tensor(lo, raw[:, slot, :], hi, ALU.subtract).then_inc(w_split, 1)

            def build_ffn_weights(layer):
                slot = (K_PIECE + layer) % RAW
                bits = raw[:, slot, :].bitcast(U8).rearrange("p (c o) -> p c o", o=E)
                dve.wait_ge(raw_loaded[slot], 16 * ((K_PIECE + layer) // RAW + 1))
                for c in range(CHUNKS):
                    scaled_part = layer > 0 and c == CHUNKS - 1
                    mul, add = (inh_mul[:, 0:1], inh_add[:, 0:1]) if scaled_part else (2.0, -1.0)
                    dve.tensor_scalar(ffn_w[layer][c], bits[:, c, :], mul, add,
                                      ALU.mult, ALU.add).then_inc(ffn_w_built, 1)

            run("prologue", -1)
            dve.wait_ge(w_split, PRO_PIECES)
            dve.wait_ge(consts, CONSTS)
            with dve.Fori(0, GROUPS - 1) as g:
                run("body", g)
            run("last", GROUPS - 1)

        @block.tensor
        def _(pe):
            def three(out, sta, mov, start, stop):
                (sta_hi, sta_lo), (mov_hi, mov_lo) = sta, mov
                pe.matmul(out, sta_hi, mov_hi, start=start, stop=False)
                pe.matmul(out, sta_hi, mov_lo, start=False, stop=False)
                return pe.matmul(out, sta_lo, mov_hi, start=False, stop=stop)

            pe.wait_ge(consts, 5)
            for _ in range(WARM_UP):
                pe.transpose(ps_t[0][:, 0, :], ident[:, :], ident[:, :])
            def run(kind, g):
                r = Run(kind, g, "pe")
                for item in r.items:
                    name = item[0]
                    bank = shared_bank(r, whole(item))
                    if name == "ln":
                        b = item[1]
                        pe.wait_ge(xn_ready, b + 1)
                        if b >= BANKS4:
                            pe.wait_ge(ln_lo, b + 1 - BANKS4)
                        for c in range(CHUNKS):
                            mm = pe.transpose(banks4[:, b % BANKS4, c * P:(c + 1) * P],
                                              x_sb[:, b, c * P:(c + 1) * P], ident[:, :])
                        mm.then_inc(ln_turned, 1)
                    elif name == "scores":
                        _, i, h = item
                        if kind == "prologue" and h == 0:
                            pe.wait_ge(ln_lo, BLOCKS)
                        if i in (0, 4):
                            pe.wait_ge(shared_read, r.shared0 + 1 + max(
                                r.order.index(("unit", p, i // 4)) for p in (f"q{h}", "k")))
                        if kind != "prologue":
                            pe.wait_ge(exp_done, r.score_no(i, h) - 1 - (HEADS * i + h)
                                       + score_exps(i, h))
                        rows = slice(i * P, (i + 1) * P)
                        banks = score_banks(i, h)
                        width = (i + 1) * P // len(banks)
                        for n, score_bank in enumerate(banks):
                            cols = slice(n * width, (n + 1) * width)
                            mm = three(banks4[:, score_bank, 0:width], (q_hi[:, h, rows], q_lo[:, h, rows]),
                                       (k_hi[:, cols], k_lo[:, cols]), True, True)
                        mm.then_inc(scores_done, 1)
                    elif name == "turn":
                        _, i, j = item
                        t = tri(i) + j
                        pe.wait_ge(turn_split, TURNS * g + t + 1)
                        if j == 0:
                            pe.wait_ge(normed, SCORES * g + HEADS * (i + 1))
                        for h in range(HEADS):
                            mm = pe.transpose(ps_t[t % TURN_RING][:, h, :],
                                              probs[i % 2][:, h, j * P:(j + 1) * P], ident[:, :])
                        mm.then_inc(turned, 1)
                    elif name == "weigh":
                        _, i, j = item
                        t = tri(i) + j
                        if (i, j) == (0, 0):
                            pe.wait_ge(shared_read, r.shared0)
                        if (i, j) == (4, 4):
                            pe.wait_ge(shared_read, r.shared_no(("vblocks", 1)))
                        if j == 0:
                            pe.wait_ge(attn_split, BLOCKS * g + i + 1)
                        pe.wait_ge(turn_split, TURNS * g + t + 1 + TURN_RING)
                        mm = three(ps_o[:, :], (v_hi[:, j, :], v_lo[:, j, :]),
                                   tuple(pt[:, t % PT_RING, :, :].rearrange("p h t -> p (h t)")
                                         for pt in (pt_hi, pt_lo)), j == 0, j == i)
                        if j == i:
                            mm.then_inc(weighed, 1)
                    elif name == "unit":
                        _, piece, half, c = item
                        no = r.shared_no(whole(item))
                        if c == 0:
                            if kind != "prologue" or no > 2:
                                pe.wait_ge(shared_read, r.bank_free(no))
                            if half == 0:
                                pe.wait_ge(w_split, r.piece_no(piece))
                        w = PIECES.index(piece)
                        if kind == "prologue" and no == 1:
                            for cols in (slice(0, HALF // 2), slice(HALF // 2, HALF)) if c == 0 else ():
                                pe.wait_ge(ln_lo, cols.stop // P)
                                for n in range(CHUNKS):
                                    mm = three(bank[:, cols], (w_hi[:, w, n, :], w_lo[:, w, n, :]),
                                               (xn_hi[:, n, cols], xn_lo[:, n, cols]),
                                               n == 0, n == CHUNKS - 1)
                        else:
                            cols = slice(half * HALF, (half + 1) * HALF)
                            mm = three(bank[:, :], (w_hi[:, w, c, :], w_lo[:, w, c, :]),
                                       (xn_hi[:, c, cols], xn_lo[:, c, cols]),
                                       c == 0, c == CHUNKS - 1)
                        if c == CHUNKS - 1:
                            mm.then_inc(shared_done, 1)
                    elif name == "vblocks":
                        half = item[1]
                        pe.wait_ge(shared_read, r.shared_no(item) - 1)
                        for n in range(4):
                            b = half * 4 + n
                            mm = pe.transpose(bank[:, n * P:(n + 1) * P], vt[:, b * P:(b + 1) * P],
                                              ident[:, :])
                        mm.then_inc(shared_done, 1)
                    elif name == "dense":
                        _, i, h = item
                        if h == 0:
                            pe.wait_ge(shared_read, r.shared_no(whole(item)) - 1)
                            pe.wait_ge(attn_split, BLOCKS * g + i + 2)
                            if i == 0:
                                pe.wait_ge(w_split, r.piece_no(f"wd{HEADS - 1}"))
                        mm = three(bank[:, :], (at_hi[:, i % ATTN_RING, h, :],
                                                at_lo[:, i % ATTN_RING, h, :]),
                                   (wd_hi[:, h, :], wd_lo[:, h, :]), h == 0, h == HEADS - 1)
                        if h == HEADS - 1:
                            mm.then_inc(shared_done, 1)
                    elif name == "final":
                        b = item[1]
                        if b == 0:
                            pe.wait_ge(ffn_w_built, CHUNKS * 3)
                            pe.wait_ge(exp_done, SCORES * GROUPS)
                        if b >= BANKS4:
                            pe.wait_ge(silu_done, b - BANKS4 + 1)
                        if b % 4 == 0:
                            pe.wait_ge(hidden_lo, HIDDEN.index(("hidden", 1, b // 4, CHUNKS - 1)) + 1)
                        for c in range(CHUNKS):
                            for part in (0, 1):
                                mm = pe.matmul(banks4[:, b % BANKS4, :],
                                               ffn_in[2][part][:, c, b * P:(b + 1) * P], ffn_w[2][c],
                                               start=(c == 0 and part == 0),
                                               stop=(c == CHUNKS - 1 and part == 1))
                        mm.then_inc(final_done, 1)
                    elif name == "hidden":
                        _, layer, half, o, c = item
                        if c == 0:
                            pe.wait_ge(shared_read, r.shared_no(whole(item)) - 1)
                            pe.wait_ge(ffn_w_built, CHUNKS * (layer + 1))
                            if layer:
                                pe.wait_ge(hidden_lo, HIDDEN.index(("hidden", 0, half, CHUNKS - 1)) + 1)
                        cols = slice(half * HALF, (half + 1) * HALF)
                        for part in (0, 1):
                            mm = pe.matmul(bank[:, :], ffn_w[layer][c][:, o * P:(o + 1) * P],
                                           ffn_in[layer][part][:, c, cols],
                                           start=(c == 0 and part == 0),
                                           stop=(c == CHUNKS - 1 and part == 1))
                        if c == CHUNKS - 1:
                            mm.then_inc(shared_done, 1)

            run("prologue", -1)
            with pe.Fori(0, GROUPS - 1) as g:
                run("body", g)
            run("last", GROUPS - 1)


def kernel(**inputs):
    import numpy as np
    import concourse.bacc as bacc
    from concourse.bass_utils import run_bass_kernel_spmd

    x = np.ascontiguousarray(inputs["L0_attn_q"]).reshape(S, E)
    w = np.asarray(inputs["L0_attn_w_qkv"])
    wq = w[:GROUPS * HEADS * P].reshape(GROUPS, HEADS, P, CHUNKS, P)
    wk = w[GROUPS * HEADS * P:][:GROUPS * P].reshape(GROUPS, 1, P, CHUNKS, P)
    wv = w[(GROUPS * HEADS + GROUPS) * P:].reshape(GROUPS, 1, P, CHUNKS, P)
    wqkv = np.ascontiguousarray(np.concatenate([wq, wv, wk], 1).transpose(0, 1, 4, 3, 2))
    wqkv = wqkv.reshape(GROUPS, PRO_PIECES, P, E)
    wd = np.ascontiguousarray(np.asarray(inputs["L0_attn_w_dense"]).T).reshape(GROUPS, HEADS, P, E)
    arrays = {"x": x, "wqkv": wqkv, "wd": wd}
    for n in range(3):
        arrays[f"k{n}"] = np.ascontiguousarray(inputs[f"L0_ffn_k{n}"])
        arrays[f"s{n}"] = np.asarray(inputs[f"L0_ffn_s{n}"]).reshape(1)

    nc = bacc.Bacc("TRN2", target_bir_lowering=False, num_devices=1)
    ap = {name: nc.dram_tensor(name, a.shape, mybir.dt.from_np(a.dtype), kind="ExternalInput").ap()
          for name, a in arrays.items()}
    out = nc.dram_tensor("out", (S, E), F32, kind="ExternalOutput").ap()
    build(nc, ap["x"], ap["wqkv"], ap["wd"], [ap[f"k{n}"] for n in range(3)],
          [ap[f"s{n}"] for n in range(3)], out)
    result = run_bass_kernel_spmd(nc, [arrays], core_ids=[0]).results[0]["out"]
    return result.reshape(1, S, E)
```
